# Optimizing a Trainium2 kernel written in Bass

```python
import numpy as np
import jax
import jax.numpy as jnp

def _softmax(x, axis=-1):
    return jax.nn.softmax(x, axis=axis)

def _gelu(x):
    return jax.nn.gelu(x, approximate=True)

def _silu(x):
    return jax.nn.silu(x)

def _sigmoid(x):
    return jax.nn.sigmoid(x)

def _layernorm(x, axis=-1, eps=1e-05):
    m = jnp.mean(x, axis=axis, keepdims=True)
    v = jnp.var(x, axis=axis, keepdims=True)
    return (x - m) / jnp.sqrt(v + eps)

def _scatter_add(tgt, idx, src, axis=0):
    return tgt.at[idx].add(src)

def _segment_sum(src, seg, n):
    return jax.ops.segment_sum(src, seg, n)
kernel_name = 'mk_prb_d1_jaxref_r8_a2c40a'

def setup_inputs(seed: int=0):
    np.random.seed(seed)
    _w = jnp.asarray

    def _L0_attn_setup():
        import jax, jax.numpy as jnp
        import numpy as np
        B, S, D = (4, 256, 128)
        COMP_RATIO = 4
        TOP_K = 64
        key = jax.random.key(seed)
        ks = jax.random.split(key, 9)
        sd = 1.0 / np.sqrt(D)
        return {'x': jax.random.normal(ks[0], (B, S, D), dtype=jnp.float32), 'Wq': jax.random.normal(ks[1], (D, D), dtype=jnp.float32) * sd, 'bq': jnp.zeros((D,), dtype=jnp.float32), 'Wk': jax.random.normal(ks[2], (D, D), dtype=jnp.float32) * sd, 'bk': jnp.zeros((D,), dtype=jnp.float32), 'Wv': jax.random.normal(ks[3], (D, D), dtype=jnp.float32) * sd, 'bv': jnp.zeros((D,), dtype=jnp.float32), 'Wo': jax.random.normal(ks[4], (D, D), dtype=jnp.float32) * sd, 'bo': jnp.zeros((D,), dtype=jnp.float32)}
    _L0_attn_in = _L0_attn_setup()

    def _L0_ffn_setup():
        import jax, jax.numpy as jnp
        import numpy as np
        DIM = 128
        HIDDEN = 384
        SCALE = 1.0 / 127.0

        def _dequant(w_int, dtype):
            return w_int.astype(dtype) * jnp.asarray(SCALE, dtype)
        key = jax.random.key(seed)
        k_x, k_g, k_u, k_d = jax.random.split(key, 4)
        x = jax.random.normal(k_x, (4, 256, DIM), dtype=jnp.float32)
        w_gate = jax.random.randint(k_g, (HIDDEN, DIM), -127, 128, dtype=jnp.int32)
        w_up = jax.random.randint(k_u, (HIDDEN, DIM), -127, 128, dtype=jnp.int32)
        w_down = jax.random.randint(k_d, (DIM, HIDDEN), -127, 128, dtype=jnp.int32)
        return {'x': x, 'w_gate': w_gate, 'w_up': w_up, 'w_down': w_down}
    _L0_ffn_in = _L0_ffn_setup()
    _d = {'L0_attn_x': _L0_attn_in['x'], 'L0_attn_Wq': _L0_attn_in['Wq'], 'L0_attn_bq': _L0_attn_in['bq'], 'L0_attn_Wk': _L0_attn_in['Wk'], 'L0_attn_bk': _L0_attn_in['bk'], 'L0_attn_Wv': _L0_attn_in['Wv'], 'L0_attn_bv': _L0_attn_in['bv'], 'L0_attn_Wo': _L0_attn_in['Wo'], 'L0_attn_bo': _L0_attn_in['bo'], 'L0_ffn_w_gate': _L0_ffn_in['w_gate'], 'L0_ffn_w_up': _L0_ffn_in['w_up'], 'L0_ffn_w_down': _L0_ffn_in['w_down']}
    _x0 = _d['L0_attn_x']
    _d['L0_attn_x'] = jax.random.normal(jax.random.fold_in(jax.random.key(seed), 1), (2, 1024, 128), dtype=_x0.dtype)
    del _x0
    return _d

def reference(L0_attn_x, L0_attn_Wq, L0_attn_bq, L0_attn_Wk, L0_attn_bk, L0_attn_Wv, L0_attn_bv, L0_attn_Wo, L0_attn_bo, L0_ffn_w_gate, L0_ffn_w_up, L0_ffn_w_down):

    def _L0_attn_ref(x, Wq, bq, Wk, bk, Wv, bv, Wo, bo):
        import jax, jax.numpy as jnp
        import numpy as np
        B, S, D = (4, 256, 128)
        COMP_RATIO = 4
        TOP_K = 64
        b, s, d = x.shape
        scale = 1.0 / jnp.sqrt(jnp.asarray(d, x.dtype))
        Q = x @ Wq + bq
        K = x @ Wk + bk
        V = x @ Wv + bv
        raw = jnp.einsum('bqd,bkd->bqk', Q, K) * scale
        causal = jnp.triu(jnp.ones((s, s), dtype=bool), k=1)
        w_scores = jnp.where(causal, jnp.asarray(-jnp.inf, raw.dtype), raw)
        w_attn = jax.nn.softmax(w_scores, axis=-1) @ V
        sc = s // COMP_RATIO
        Kc = K.reshape(b, sc, COMP_RATIO, d).mean(axis=2)
        Vc = V.reshape(b, sc, COMP_RATIO, d).mean(axis=2)
        c_scores = jnp.einsum('bqd,bkd->bqk', Q, Kc) * scale
        c_attn = jax.nn.softmax(c_scores, axis=-1) @ Vc
        top_vals, top_idx = jax.lax.top_k(raw, TOP_K)
        bi = jnp.arange(b)[:, None, None]
        si = jnp.arange(s)[None, :, None]
        sparse = jnp.zeros_like(raw).at[bi, si, top_idx].set(top_vals)
        s_attn = jax.nn.softmax(sparse, axis=-1) @ V
        out = (w_attn + c_attn + s_attn) / 3.0
        return out @ Wo + bo

    def _L0_ffn_ref(x, w_gate, w_up, w_down):
        import jax, jax.numpy as jnp
        import numpy as np
        DIM = 128
        HIDDEN = 384
        SCALE = 1.0 / 127.0

        def _dequant(w_int, dtype):
            return w_int.astype(dtype) * jnp.asarray(SCALE, dtype)
        wg = _dequant(w_gate, x.dtype)
        wu = _dequant(w_up, x.dtype)
        wd = _dequant(w_down, x.dtype)
        gate = jnp.einsum('bsd,hd->bsh', x, wg)
        up = jnp.einsum('bsd,hd->bsh', x, wu)
        h = jax.nn.silu(gate) * up
        return jnp.einsum('bsh,dh->bsd', h, wd)
    x = L0_attn_x
    xn = _layernorm(x, axis=-1)
    x = x + _L0_attn_ref(xn, L0_attn_Wq, L0_attn_bq, L0_attn_Wk, L0_attn_bk, L0_attn_Wv, L0_attn_bv, L0_attn_Wo, L0_attn_bo) + _L0_ffn_ref(xn, L0_ffn_w_gate, L0_ffn_w_up, L0_ffn_w_down)
    return x

_drawn_inputs = setup_inputs


def setup_inputs(seed=0):
    import zlib

    import numpy as np

    out = dict(_drawn_inputs(seed))
    spreads = {'L0_attn_bq': (0.0, 0.8),
     'L0_attn_bk': (0.0, 2.0),
     'L0_attn_bv': (0.0, 2.0),
     'L0_attn_bo': (0.0, 2.0)}
    factors = {'L0_attn_Wq': 8.0, 'L0_attn_Wk': 8.0, 'L0_attn_Wv': 8.0, 'L0_attn_Wo': 8.0}
    for name, (base, spread) in spreads.items():
        noise = np.random.default_rng([zlib.crc32(name.encode()), seed]).standard_normal(out[name].shape)
        drawn = base * np.exp(spread * noise) if base else spread * noise
        out[name] = jnp.asarray(drawn.astype(out[name].dtype))
    for name, factor in factors.items():
        out[name] = (out[name] * factor).astype(out[name].dtype)
    return out
```

```python
from contextlib import ExitStack
from math import erf, exp, pi, sqrt

import concourse.bass as bass
from concourse import mybir

ALU = mybir.AluOpType
ACT = mybir.ActivationFunctionType
F32 = mybir.dt.float32
BF16 = mybir.dt.bfloat16
I32 = mybir.dt.int32
AX_X = mybir.AxisListType.X

P = 128
TOP_K = 64
COMP = 4
EPS = 1e-5
TINY = 2.0 ** -60
MASKED = -3.0e38
LOWEST = -3.4e38


def normal_quantile(share):
    low, high = -8.0, 8.0
    for _ in range(60):
        z = (low + high) / 2
        low, high = (z, high) if 0.5 * (1 + erf(z / sqrt(2))) < share else (low, z)
    return z


def attention_ffn_block(nc, x, wq, bq, wk, bk, wv, bv, wo, bo, w_gate, w_up, w_down, out):
    B, S, D = x.shape
    H = w_gate.shape[0]
    NT = B * S // P
    TB = S // P
    CT = 4
    NC = NT // CT
    CB = TB // CT
    CW = CT * P
    NH = H // P
    SC = S // COMP
    CC = SC // P
    HALF = S // 2
    SCALE = 1.0 / sqrt(D)
    DEQUANT = 1.0 / 127.0
    assert D == P and HALF == 512 and CT * P == 512 and S % 512 == 0

    z_top = normal_quantile(1.0 - TOP_K / S)
    per_count = sqrt(2 * pi) * exp(z_top * z_top / 2) / S
    STEPS = (1.0, 0.5)
    MID = S / 2 - TOP_K

    with ExitStack() as ctx:
        def sb(name, shape, dt=F32):
            return ctx.enter_context(nc.sbuf_tensor(name, shape, dt))

        def sem(name):
            return ctx.enter_context(nc.semaphore(name))

        score_bank = [ctx.enter_context(nc.psum_tensor(f"score{h}", [P, HALF], F32)) for h in range(2)]
        comp_bank = ctx.enter_context(nc.psum_tensor("comp_bank", [P, 512], F32))
        NW = 5
        work_bank = [ctx.enter_context(nc.psum_tensor(f"work{i}", [P, 512], F32)) for i in range(NW)]

        XR = 8
        ident = sb("ident", [P, P])
        causal = sb("causal", [P, P])
        ones = sb("ones", [P, 1])
        ramp = sb("ramp", [P, 2, 9])
        half_pow = sb("half_pow", [P, 2, CT])
        x_in = sb("x_in", [P, NT, D])
        xn = sb("xn", [P, NT, D])
        xnT = sb("xnT", [P, NT * P])
        w_in = sb("w_in", [P, 4, D])
        b_in = sb("b_in", [P, 3])
        bo_rows = sb("bo_rows", [P, D])
        wi_gate = sb("wi_gate", [P, NH, D], I32)
        wi_up = sb("wi_up", [P, NH, D], I32)
        wi_down = sb("wi_down", [P, H], I32)
        wf_gate = sb("wf_gate", [P, NH, D])
        wf_up = sb("wf_up", [P, NH, D])
        wf_down = sb("wf_down", [P, H])
        wT_gate = sb("wT_gate", [P, H])
        wT_up = sb("wT_up", [P, H])
        wT_down = sb("wT_down", [P, NH, D])
        bn = sb("bn", [P, NT, 6])
        mv = sb("mv", [P, NT, 2])
        rstd = sb("rstd", [P, NT])
        ln_tmp = sb("ln_tmp", [P, 3, CT])
        qT = sb("qT", [P, NT * P])
        kT = sb("kT", [P, NT * P])
        vT = sb("vT", [P, NT * P])
        kcT = sb("kcT", [P, B * SC])
        vcT = sb("vcT", [P, B * SC])
        ksum = sb("ksum", [P, NC])
        kbar = sb("kbar", [P, B])
        mom = sb("mom", [P, 3, D])
        qcq = sb("qcq", [P, CW])
        vo = sb("vo", [P, NT, D])
        vco = sb("vco", [P, B * CC, D])
        mu_var = sb("mu_var", [P, NT, 2])
        nslope = sb("nslope", [P, 2, NT])
        nthr = sb("nthr", [P, 3, NT])
        nthr_off = sb("nthr_off", [P, 2, NT])
        thr_tmp = sb("thr_tmp", [P, 2, CT])
        signs = sb("signs", [P, 3, NT])
        scores = sb("scores", [P, XR, S])
        comp = sb("comp", [P, XR, SC])
        sg_skip = sb("sg_skip", [P, S], BF16)
        sg = sb("sg", [P, 4, S], BF16)
        near = sb("near", [P, S])
        m9 = sb("m9", [P, NT, 9])
        far = sb("far", [P, NT])
        d_off = sb("d_off", [P, NT])
        side = sb("side", [P, NT])
        nside = sb("nside", [P, NT])
        dist = sb("dist", [P, NT])
        pick = sb("pick", [P, NT])
        hot = sb("hot", [P, 2, 9])
        hot8 = sb("hot8", [P, 2, 8])
        gaps = sb("gaps", [P, 2, 8])
        tau = sb("tau", [P, NT])
        good = sb("good", [P, NT])
        gap = sb("gap", [P, NT])
        tied = sb("tied", [P, NT])
        n_good = sb("n_good", [1, NT // 2])
        n_good_i = sb("n_good_i", [1, NT // 2], I32)
        taken = sb("taken", [P, S])
        maxes = sb("maxes", [P, NT, 5])
        nmax = sb("nmax", [P, NT, 3])
        zsum = sb("zsum", [P, NT, 3])
        zinv = sb("zinv", [P, NT, 3])
        ratio = sb("ratio", [P, NT, 2])
        p_sparse = sb("p_sparse", [P, 4, S])
        p_causal = sb("p_causal", [P, 2, S])
        p_comp = sb("p_comp", [P, 2, SC])
        pT = sb("pT", [P, 2, S + SC])
        tanh_g = sb("tanh_g", [P, 2, CW])
        gated = sb("gated", [P, CW])
        hid = sb("hid", [P, 2, NH, CW])
        base = x_in

        x_loaded = [sem(f"x_loaded{c}") for c in range(NC)]
        w_loaded = sem("w_loaded")
        wvo_loaded = sem("wvo_loaded")
        ffn_w_loaded = sem("ffn_w_loaded")
        bo_loaded = sem("bo_loaded")
        ident_ready = sem("ident_ready")
        pool_step = sem("pool_step")
        const_ready = sem("const_ready")
        vec_step = sem("vec_step")
        stats_ready = sem("stats_ready")
        rstd_ready = sem("rstd_ready")
        xn_ready = sem("xn_ready")
        w_float = sem("w_float")
        filled = [sem(f"work_filled{i}") for i in range(NW)]
        drained = [sem(f"work_drained{i}") for i in range(NW)]
        kc_ready = sem("kc_ready")
        vc_ready = sem("vc_ready")
        kbar_ready = sem("kbar_ready")
        half_filled = [sem(f"half_filled{h}") for h in range(2)]
        half_drained = [sem(f"half_drained{h}") for h in range(2)]
        comp_filled = sem("comp_filled")
        comp_drained = sem("comp_drained")
        thr_ready = [sem(f"thr_ready{r}") for r in range(3)]
        counted = [sem(f"counted{r}") for r in range(3)]
        flip_done = sem("flip_done")
        near_max = sem("near_max")
        good_ready = sem("good_ready")
        checked = sem("checked")
        check_read = sem("check_read")
        sparse_ready = sem("sparse_ready")
        nmax_ready = sem("nmax_ready")
        exp_sparse = sem("exp_sparse")
        exp_causal = sem("exp_causal")
        exp_comp = sem("exp_comp")
        zinv_ready = sem("zinv_ready")
        mixed = sem("mixed")
        tanh_ready = sem("tanh_ready")
        xb_ready = sem("xb_ready")
        base_ready = sem("base_ready")
        stored = sem("stored")

        schedule = [("consts",), ("ln", 0), ("ln", 1), ("xnT", 0), ("xnT", 1), ("K", 0), ("K", 1), ("Q", 0),
                    ("kbar", 0), ("moment", 0), ("comp_k", 0), ("comp_k", 1), ("guess", 0), ("raw", 0),
                    ("V", 0), ("V", 1), ("comp_v", 0), ("comp_v", 1)]
        extra = {
            0: [("Q", 1), ("guess", 1), ("ffn_weights",), ("xb", 0)],
            1: [("ffn", 0, 0), ("ffn", 0, 1), ("ln", 2)],
            2: [("ffn", 0, 2), ("down", 0), ("ln", 3), ("xnT", 2)],
            3: [("vo", 0), ("vo", 1), ("vco", 0), ("xb", 1), ("ffn", 1, 0), ("xnT", 3)],
            4: [("K", 2), ("K", 3), ("Q", 2), ("comp_k", 2), ("ffn", 1, 1), ("kbar", 1), ("moment", 1)],
            5: [("ffn", 1, 2), ("down", 1), ("comp_k", 3), ("guess", 2), ("xb", 2)],
            6: [("V", 2), ("Q", 3), ("guess", 3)],
            7: [("V", 3), ("comp_v", 2), ("ffn", 2, 0)],
            8: [("comp_v", 3), ("vo", 2), ("vo", 3), ("vco", 1)],
            9: [("ffn", 2, 1)],
            10: [("ffn", 2, 2), ("down", 2), ("xb", 3)],
            11: [("ffn", 3, 0)],
            12: [("ffn", 3, 1)],
            13: [("ffn", 3, 2), ("down", 3)],
        }
        LAG = 4
        for i in range(NT + LAG + 2):
            t = i - LAG
            if i + 1 < NT:
                schedule.append(("raw", i + 1))
            if i % 2 == 0 and 0 <= i - 2 < NT:
                schedule.append(("choose_side", (i - 2) // 2))
            if i < NT:
                schedule.append(("count", 0, i))
            if 0 <= i - 2 < NT:
                schedule.append(("neighbours", i - 2))
            if 0 <= t < NT:
                schedule.append(("softmax", t, 2))
            if i < NT:
                schedule.append(("count", 1, i))
            if 0 <= t < NT:
                schedule.append(("softmax", t, 0))
            if 0 <= t - 1 < NT:
                schedule.append(("turn", t - 1))
            schedule += extra.get(i, [])
            if i < NT:
                schedule.append(("count", 2, i))
            if 0 <= t < NT:
                schedule.append(("softmax", t, 1))
                schedule.append(("mix", t))
            if i % 2 == 1 and 0 <= i - 3 < NT:
                schedule.append(("choose", (i - 3) // 2))
            if i % 2 == 1 and 0 <= i - 3 < NT:
                schedule += [("sparse", (i - 3) // 2)]
            if 0 <= t - 1 < NT:
                schedule.append(("attend", t - 1))
                schedule.append(("finish", t - 1))

        jobs = {}

        def job(*name):
            jobs[name] = (len(jobs) % NW, len(jobs) // NW + 1)

        for stage, *a in schedule:
            if stage == "xnT":
                job("xnT", *a)
            elif stage in ("Q", "K", "V", "vo", "vco", "down"):
                job(stage, *a)
            elif stage == "moment":
                for n in range(3):
                    job("moment", a[0], n)
            elif stage == "guess":
                job("cq", *a)
                job("muvar", *a)
            elif stage == "ffn_weights":
                for n in range(3):
                    job("wT", n)
            elif stage == "ffn":
                job("gate", *a)
                job("up", *a)
            elif stage == "choose":
                job("check", *a)
            elif stage == "turn":
                for n in range(3):
                    job("turn", a[0], n)
            elif stage == "attend":
                job("attend", *a)

        def bank(*name):
            return work_bank[jobs[name][0]]

        def acquire(pe, *name):
            b, n = jobs[name]
            if n > 1:
                pe.wait_ge(drained[b], n - 1)

        def fill_sem(*name):
            return filled[jobs[name][0]]

        def drain_sem(*name):
            return drained[jobs[name][0]]

        def await_fill(eng, *name):
            eng.wait_ge(filled[jobs[name][0]], jobs[name][1])

        def await_drain(eng, *name):
            eng.wait_ge(drained[jobs[name][0]], jobs[name][1])

        def causal_width(t):
            return (t % TB + 1) * P

        def pieces(t):
            cut = (t % TB) * P
            ends = sorted({0, cut, HALF, S})
            return [(a, b) for a, b in zip(ends[:-1], ends[1:])]

        x_v = x.rearrange("b (c j p) d -> (b c) p j d", p=P, j=CT)
        out_v = out.rearrange("b (t p) d -> (b t) p d", p=P)
        block = ctx.enter_context(nc.Block())

        @block.sync
        def _(sp):
            for c in range(CB):
                sp.dma_start(x_in[:, c * CT:(c + 1) * CT, :], x_v[c]).then_inc(x_loaded[c], 16)
            for i, w in ((1, wk), (0, wq)):
                sp.dma_start(w_in[:, i, :], w).then_inc(w_loaded, 16)
            for i, b in enumerate((bq, bk, bv)):
                sp.dma_start(b_in[:, i:i + 1], b.unsqueeze(1)).then_inc(w_loaded, 16)
            for i, w in ((2, wv), (3, wo)):
                sp.dma_start(w_in[:, i, :], w).then_inc(wvo_loaded, 16)
            sp.dma_start(wi_gate[:, :, :], w_gate.rearrange("(n p) d -> p n d", p=P)).then_inc(ffn_w_loaded, 16)
            sp.dma_start(wi_up[:, :, :], w_up.rearrange("(n p) d -> p n d", p=P)).then_inc(ffn_w_loaded, 16)
            sp.dma_start(wi_down[:, :], w_down).then_inc(ffn_w_loaded, 16)
            sp.dma_start(bo_rows[:, :], bo.unsqueeze(0).to_broadcast([P, D])).then_inc(bo_loaded, 16)
            for c in range(CB, NC):
                sp.dma_start(x_in[:, c * CT:(c + 1) * CT, :], x_v[c]).then_inc(x_loaded[c], 16)
            for t in range(NT):
                await_drain(sp, "attend", t)
                sp.dma_start(out_v[t], base[:, t, :]).then_inc(stored, 16)
            sp.wait_ge(stored, 16 * NT)

        @block.gpsimd
        def _(pool):
            g = nc.gpsimd
            steps = [0]

            def chain(ins):
                steps[0] += 1
                ins.then_inc(pool_step, 1)
                pool.wait_ge(pool_step, steps[0])

            def consts():
                chain(g.memset(ident[:], 0.0))
                g.affine_select(out=ident[:], in_=ident[:], compare_op=ALU.not_equal, fill=1.0, base=0,
                                pattern=[[-1, P]], channel_multiplier=1).then_inc(ident_ready, 1)
                chain(g.memset(causal[:], 0.0))
                g.affine_select(out=causal[:], in_=causal[:], compare_op=ALU.is_ge, fill=MASKED, base=0,
                                pattern=[[-1, P]], channel_multiplier=1).then_inc(ident_ready, 1)

            def ln(c):
                v, a, r = ln_tmp[:, 0, :], ln_tmp[:, 1, :], ln_tmp[:, 2, :]
                pool.wait_ge(stats_ready, c + 1)
                if c == 0:
                    pool.wait_ge(const_ready, 1)
                chain(g.tensor_scalar(v, mv[:, c * CT:(c + 1) * CT, 1], EPS, None, ALU.add))
                chain(g.tensor_tensor(r, v, half_pow[:, 0, :], ALU.pow))
                chain(g.tensor_tensor(a, r, r, ALU.mult))
                chain(g.tensor_tensor(a, a, v, ALU.mult))
                chain(g.tensor_scalar(a, a, -0.5, 1.5, ALU.mult, ALU.add))
                g.tensor_tensor(rstd[:, c * CT:(c + 1) * CT], r, a, ALU.mult).then_inc(rstd_ready, 1)

            def guess(c):
                ts = slice(c * CT, (c + 1) * CT)
                dev, off = thr_tmp[:, 0, :], thr_tmp[:, 1, :]
                await_drain(pool, "muvar", c)
                chain(g.tensor_scalar(dev, mu_var[:, ts, 1], 1e-30, None, ALU.max))
                chain(g.tensor_tensor(dev, dev, half_pow[:, 1, :], ALU.pow))
                for r in range(2):
                    g.tensor_scalar(nslope[:, r, ts], dev, -per_count * STEPS[r] / 2, None, ALU.mult).then_inc(pool_step, 1)
                    steps[0] += 1
                pool.wait_ge(pool_step, steps[0])
                chain(g.tensor_scalar(dev, dev, -z_top, None, ALU.mult))
                chain(g.tensor_tensor(nthr[:, 0, ts], dev, mu_var[:, ts, 0], ALU.subtract))
                chain(g.tensor_scalar(off, nslope[:, 0, ts], 2 * MID, None, ALU.mult))
                g.tensor_tensor(nthr_off[:, 0, ts], off, nthr[:, 0, ts], ALU.add).then_inc(thr_ready[0], 1)

            def count(r, t):
                if r == 2:
                    return
                col = slice(t, t + 1)
                pool.wait_ge(counted[r], t + 1)
                nxt = g.tensor_scalar(nthr[:, r + 1, col], signs[:, r, col], nslope[:, r, col], nthr_off[:, r, col],
                                      ALU.mult, ALU.add)
                nxt.then_inc(thr_ready[r + 1], 1)
                if r == 0:
                    pool.wait_ge(thr_ready[1], t + 1)
                    chain(g.tensor_scalar(nthr_off[:, 1, col], nslope[:, 1, col], 2 * MID, nthr[:, 1, col],
                                          ALU.mult, ALU.add))

            def mix(t):
                w = causal_width(t)
                pool.wait_ge(zinv_ready, t + 1)
                chain(g.tensor_scalar(ratio[:, t, :], zinv[:, t, 0:2], zsum[:, t, 2:3], 1.0, ALU.mult, ALU.mult))
                pc, pw, ps = p_comp[:, t % 2, :], p_causal[:, t % 2, 0:w], p_sparse[:, t % 4, 0:w]
                g.tensor_scalar(pc, pc, ratio[:, t, 1:2], 1.0, ALU.mult, ALU.mult)
                chain(g.tensor_scalar(pw, pw, ratio[:, t, 0:1], 1.0, ALU.mult, ALU.mult))
                g.tensor_tensor(ps, ps, pw, ALU.add).then_inc(mixed, 1)

            def xb(c):
                ts = slice(c * CT, (c + 1) * CT)
                pool.wait_ge(xn_ready, (c + 1) * CT)
                pool.wait_ge(bo_loaded, 16)
                g.tensor_tensor(base[:, ts, :], x_in[:, ts, :], bo_rows[:, :].unsqueeze(1).to_broadcast([P, CT, D]),
                                ALU.add).then_inc(xb_ready, 1)

            own = {"consts": consts, "ln": ln, "guess": guess, "count": count, "mix": mix, "xb": xb}
            for stage, *a in schedule:
                if stage in own:
                    own[stage](*a)

        @block.tensor
        def _(pe):
            mm = nc.tensor.matmul

            def turned(dst, src):
                return mm(dst, src, ident[:], start=True, stop=True, is_transpose=True)

            def xnT_(c):
                acquire(pe, "xnT", c)
                if c == 0:
                    pe.wait_ge(ident_ready, 1)
                for j in range(CT):
                    pe.wait_ge(xn_ready, c * CT + j + 1)
                    last = turned(bank("xnT", c)[:, j * P:(j + 1) * P], xn[:, c * CT + j, :])
                last.then_inc(fill_sem("xnT", c), 1)

            def project(name, i, c):
                acquire(pe, name, c)
                pe.wait_ge(*((wvo_loaded, 32) if i == 2 else (w_loaded, 80)))
                await_drain(pe, "xnT", c)
                mm(bank(name, c)[:, :], w_in[:, i, :], xnT[:, c * CW:(c + 1) * CW], start=True,
                   stop=True).then_inc(fill_sem(name, c), 1)

            def moment(b):
                acquire(pe, "moment", b, 0)
                pe.wait_ge(xn_ready, (b + 1) * TB)
                for j in range(TB):
                    last = mm(bank("moment", b, 0)[:, 0:D], xn[:, b * TB + j, :], xn[:, b * TB + j, :],
                              start=(j == 0), stop=(j == TB - 1))
                last.then_inc(fill_sem("moment", b, 0), 1)
                acquire(pe, "moment", b, 1)
                await_drain(pe, "moment", b, 0)
                mm(bank("moment", b, 1)[:, 0:D], mom[:, 0, :], w_in[:, 1, :], start=True,
                   stop=True).then_inc(fill_sem("moment", b, 1), 1)
                acquire(pe, "moment", b, 2)
                await_drain(pe, "moment", b, 1)
                mm(bank("moment", b, 2)[:, 0:D], w_in[:, 1, :], mom[:, 1, :], start=True,
                   stop=True).then_inc(fill_sem("moment", b, 2), 1)

            def guess(c):
                acquire(pe, "cq", c)
                await_drain(pe, "moment", c // CB, 2)
                await_drain(pe, "Q", c)
                mm(bank("cq", c)[:, :], mom[:, 2, :], qT[:, c * CW:(c + 1) * CW], start=True,
                   stop=True).then_inc(fill_sem("cq", c), 1)
                acquire(pe, "muvar", c)
                pe.wait_ge(kbar_ready, c // CB + 1)
                pe.wait_ge(const_ready, 1)
                await_drain(pe, "cq", c)
                for j in range(CT):
                    mm(bank("muvar", c)[:, 2 * j:2 * j + 1], qT[:, c * CW + j * P:c * CW + (j + 1) * P],
                       kbar[:, c // CB:c // CB + 1], start=True, stop=True)
                    last = mm(bank("muvar", c)[:, 2 * j + 1:2 * j + 2], qcq[:, j * P:(j + 1) * P], ones[:, 0:1],
                              start=True, stop=True)
                last.then_inc(fill_sem("muvar", c), 1)

            def raw(t):
                b, q = t // TB, qT[:, t * P:(t + 1) * P]
                await_drain(pe, "Q", t // CT)
                for h in range(2):
                    await_drain(pe, "K", b * CB + h)
                    if t >= 1:
                        pe.wait_ge(half_drained[h], t)
                    mm(score_bank[h][:, :], q, kT[:, b * S + h * HALF:b * S + (h + 1) * HALF], start=True,
                       stop=True).then_inc(half_filled[h], 1)
                if t >= 1:
                    pe.wait_ge(comp_drained, t)
                pe.wait_ge(kc_ready, (b + 1) * CB)
                mm(comp_bank[:, 0:SC], q, kcT[:, b * SC:(b + 1) * SC], start=True, stop=True).then_inc(comp_filled, 1)

            def vo_(c):
                acquire(pe, "vo", c)
                await_drain(pe, "V", c)
                for j in range(CT):
                    last = mm(bank("vo", c)[:, j * D:(j + 1) * D], vT[:, c * CW + j * P:c * CW + (j + 1) * P],
                              w_in[:, 3, :], start=True, stop=True)
                last.then_inc(fill_sem("vo", c), 1)

            def vco_(b):
                acquire(pe, "vco", b)
                pe.wait_ge(vc_ready, (b + 1) * CB)
                for j in range(CC):
                    last = mm(bank("vco", b)[:, j * D:(j + 1) * D], vcT[:, b * SC + j * P:b * SC + (j + 1) * P],
                              w_in[:, 3, :], start=True, stop=True)
                last.then_inc(fill_sem("vco", b), 1)

            def ffn_weights():
                for n, w in enumerate((wf_gate, wf_up, wf_down)):
                    acquire(pe, "wT", n)
                    pe.wait_ge(w_float, n + 1)
                    for j in range(NH):
                        src = w[:, j * P:(j + 1) * P] if n == 2 else w[:, j, :]
                        last = turned(bank("wT", n)[:, j * P:(j + 1) * P], src)
                    last.then_inc(fill_sem("wT", n), 1)

            def ffn(c, h):
                for n in range(2):
                    await_drain(pe, "wT", n)
                await_drain(pe, "xnT", c)
                for name, w in (("gate", wT_gate), ("up", wT_up)):
                    acquire(pe, name, c, h)
                    mm(bank(name, c, h)[:, :], w[:, h * P:(h + 1) * P], xnT[:, c * CW:(c + 1) * CW], start=True,
                       stop=True).then_inc(fill_sem(name, c, h), 1)

            def down(c):
                acquire(pe, "down", c)
                await_drain(pe, "wT", 2)
                for h in range(NH):
                    await_drain(pe, "up", c, h)
                for j in range(CT):
                    for h in range(NH):
                        last = mm(bank("down", c)[:, j * D:(j + 1) * D], hid[:, c % 2, h, j * P:(j + 1) * P],
                                  wT_down[:, h, :], start=(h == 0), stop=(h == NH - 1))
                last.then_inc(fill_sem("down", c), 1)

            def choose(p):
                acquire(pe, "check", p)
                pe.wait_ge(good_ready, p + 1)
                mm(bank("check", p)[0:1, 0:2], ones[:, 0:1], good[:, 2 * p:2 * p + 2], start=True,
                   stop=True).then_inc(fill_sem("check", p), 1)

            def turn(t):
                pe.wait_ge(mixed, t + 1)
                for n in range(3):
                    acquire(pe, "turn", t, n)
                    for j in range(CC if n == 2 else CT):
                        src = p_comp[:, t % 2, j * P:(j + 1) * P] if n == 2 else \
                            p_sparse[:, t % 4, (n * CT + j) * P:(n * CT + j + 1) * P]
                        last = turned(bank("turn", t, n)[:, j * P:(j + 1) * P], src)
                    last.then_inc(fill_sem("turn", t, n), 1)

            def attend(t):
                b = t // TB
                acquire(pe, "attend", t)
                for c in range(b * CB, (b + 1) * CB):
                    await_drain(pe, "vo", c)
                await_drain(pe, "vco", b)
                for n in range(3):
                    await_drain(pe, "turn", t, n)
                    for j in range(CC if n == 2 else CT):
                        k = n * CT + j
                        v = vco[:, b * CC + j, :] if n == 2 else vo[:, b * TB + k, :]
                        last = mm(bank("attend", t)[:, 0:D], pT[:, t % 2, k * P:(k + 1) * P], v,
                                  start=(k == 0), stop=(k == TB + CC - 1))
                last.then_inc(fill_sem("attend", t), 1)

            own = {"xnT": xnT_, "Q": lambda c: project("Q", 0, c), "K": lambda c: project("K", 1, c),
                   "V": lambda c: project("V", 2, c), "moment": moment, "guess": guess, "raw": raw, "vo": vo_,
                   "vco": vco_, "ffn_weights": ffn_weights, "ffn": ffn, "down": down, "choose": choose,
                   "turn": turn, "attend": attend}
            for stage, *a in schedule:
                if stage in own:
                    own[stage](*a)

        @block.scalar
        def _(act):
            a_ = nc.scalar.activation

            def xnT_(c):
                await_fill(act, "xnT", c)
                a_(xnT[:, c * CW:(c + 1) * CW], bank("xnT", c)[:, :], ACT.Copy).then_inc(drain_sem("xnT", c), 1)

            def K(c):
                await_fill(act, "K", c)
                act.wait_ge(w_loaded, 16 * 5)
                a_(kT[:, c * CW:(c + 1) * CW], bank("K", c)[:, :], ACT.Identity, bias=b_in[:, 1:2],
                   accum_out=ksum[:, c:c + 1]).then_inc(drain_sem("K", c), 1)

            def V(c):
                await_fill(act, "V", c)
                act.wait_ge(w_loaded, 16 * 5)
                a_(vT[:, c * CW:(c + 1) * CW], bank("V", c)[:, :], ACT.Identity,
                   bias=b_in[:, 2:3]).then_inc(drain_sem("V", c), 1)

            def vo_(c):
                await_fill(act, "vo", c)
                a_(vo[:, c * CT:(c + 1) * CT, :], bank("vo", c)[:, :].rearrange("p (j d) -> p j d", d=D), ACT.Copy,
                   scale=1.0 / 3.0).then_inc(drain_sem("vo", c), 1)

            def vco_(b):
                await_fill(act, "vco", b)
                a_(vco[:, b * CC:(b + 1) * CC, :], bank("vco", b)[:, 0:CC * D].rearrange("p (j d) -> p j d", d=D),
                   ACT.Copy, scale=1.0 / (3.0 * COMP)).then_inc(drain_sem("vco", b), 1)

            def count(r, t):
                if r == 0:
                    act.wait_ge(half_drained[0], t + 1)
                    act.wait_ge(half_drained[1], t + 1)
                    act.wait_ge(thr_ready[0], t // CT + 1)
                else:
                    act.wait_ge(thr_ready[r], t + 1)
                if r == 2 and t >= 4:
                    act.wait_ge(near_max, t - 3)
                dst = sg[:, t % 4, :] if r == 2 else sg_skip[:, :]
                a_(dst, scores[:, t % XR, :], ACT.Sign, bias=nthr[:, r, t:t + 1], scale=1.0,
                   accum_out=signs[:, r, t:t + 1]).then_inc(counted[r], 1)

            def softmax(t, which):
                w = causal_width(t)
                if which == 2:
                    act.wait_ge(sparse_ready, t + 1)
                    act.wait_ge(nmax_ready, t + 1)
                    a_(p_sparse[:, t % 4, :], p_sparse[:, t % 4, :], ACT.Exp, bias=nmax[:, t, 2:3],
                       accum_out=zsum[:, t, 2:3]).then_inc(exp_sparse, 1)
                elif which == 0:
                    if t >= 2:
                        await_fill(act, "turn", t - 2, 2)
                    a_(p_causal[:, t % 2, 0:w], scores[:, t % XR, 0:w], ACT.Exp, bias=nmax[:, t, 0:1],
                       accum_out=zsum[:, t, 0:1]).then_inc(exp_causal, 1)
                else:
                    a_(p_comp[:, t % 2, :], comp[:, t % XR, :], ACT.Exp, bias=nmax[:, t, 1:2], scale=-1.0,
                       accum_out=zsum[:, t, 1:2]).then_inc(exp_comp, 1)

            def turn(t):
                if t >= 2:
                    await_fill(act, "attend", t - 2)
                for n in (0, 2):
                    await_fill(act, "turn", t, n)
                    w = CC * P if n == 2 else CT * P
                    a_(pT[:, t % 2, n * CT * P:n * CT * P + w], bank("turn", t, n)[:, 0:w],
                       ACT.Copy).then_inc(drain_sem("turn", t, n), 1)

            def ffn(c, h):
                n = c * NH + h
                await_fill(act, "gate", c, h)
                if n >= 2:
                    await_drain(act, "gate", (n - 2) // NH, (n - 2) % NH)
                a_(tanh_g[:, n % 2, :], bank("gate", c, h)[:, :], ACT.Tanh, scale=0.5).then_inc(tanh_ready, 1)

            own = {"xnT": xnT_, "K": K, "V": V, "vo": vo_, "vco": vco_, "count": count, "softmax": softmax,
                   "turn": turn, "ffn": ffn}
            for stage, *a in schedule:
                if stage in own:
                    own[stage](*a)

        @block.vector
        def _(dve):
            v = nc.vector
            steps = [0]

            def mark(ins):
                steps[0] += 1
                ins.then_inc(vec_step, 1)
                return steps[0]

            def chain(ins):
                dve.wait_ge(vec_step, mark(ins))

            def consts():
                v.memset(half_pow[:, 0, :], -0.5)
                v.memset(half_pow[:, 1, :], 0.5)
                v.memset(maxes[:, :, :], 0.0)
                for j in range(9):
                    v.memset(ramp[:, :, j:j + 1], float(j))
                v.memset(ones[:, :], 1.0).then_inc(const_ready, 1)
                dve.wait_ge(const_ready, 1)

            def ln(c):
                dve.wait_ge(x_loaded[c], 16)
                for t in range(c * CT, (c + 1) * CT):
                    last = v.bn_stats(bn[:, t, :], x_in[:, t, :])
                chain(last)
                for t in range(c * CT, (c + 1) * CT):
                    last = v.bn_aggr(mv[:, t, :], bn[:, t, :])
                last.then_inc(stats_ready, 1)
                dve.wait_ge(rstd_ready, c + 1)
                for t in range(c * CT, (c + 1) * CT):
                    v.tensor_scalar(xn[:, t, :], x_in[:, t, :], mv[:, t, 0:1], rstd[:, t:t + 1], ALU.subtract,
                                    ALU.mult).then_inc(xn_ready, 1)

            def Q(c):
                await_fill(dve, "Q", c)
                dve.wait_ge(w_loaded, 16 * 5)
                v.tensor_scalar(qT[:, c * CW:(c + 1) * CW], bank("Q", c)[:, :], b_in[:, 0:1], SCALE, ALU.add,
                                ALU.mult).then_inc(drain_sem("Q", c), 1)

            def kbar_(b):
                for c in range(b * CB, (b + 1) * CB):
                    await_drain(dve, "K", c)
                chain(v.tensor_reduce(kbar[:, b:b + 1], ksum[:, b * CB:(b + 1) * CB], AX_X, ALU.add))
                v.tensor_scalar(kbar[:, b:b + 1], kbar[:, b:b + 1], 1.0 / S, None, ALU.mult).then_inc(kbar_ready, 1)

            def moment(b):
                for n in range(3):
                    await_fill(dve, "moment", b, n)
                    if n == 2 and b:
                        await_fill(dve, "cq", b * CB - 1)
                    v.tensor_scalar(mom[:, n, :], bank("moment", b, n)[:, 0:D], 1.0 / S if n == 0 else 1.0, None,
                                    ALU.mult).then_inc(drain_sem("moment", b, n), 1)

            def guess(c):
                await_fill(dve, "cq", c)
                if c >= 1:
                    await_fill(dve, "muvar", c - 1)
                v.tensor_tensor(qcq[:, :], bank("cq", c)[:, :], qT[:, c * CW:(c + 1) * CW],
                                ALU.mult).then_inc(drain_sem("cq", c), 1)
                await_fill(dve, "muvar", c)
                v.tensor_copy(mu_var[:, c * CT:(c + 1) * CT, :],
                              bank("muvar", c)[:, 0:2 * CT].rearrange("p (j s) -> p j s", s=2)
                              ).then_inc(drain_sem("muvar", c), 1)

            def comp_k(c):
                await_drain(dve, "K", c)
                v.tensor_reduce(kcT[:, c * P:(c + 1) * P],
                                kT[:, c * CW:(c + 1) * CW].rearrange("p (n r) -> p n r", r=COMP), AX_X,
                                ALU.add).then_inc(kc_ready, 1)

            def comp_v(c):
                await_drain(dve, "V", c)
                v.tensor_reduce(vcT[:, c * P:(c + 1) * P],
                                vT[:, c * CW:(c + 1) * CW].rearrange("p (n r) -> p n r", r=COMP), AX_X,
                                ALU.add).then_inc(vc_ready, 1)

            def raw(t):
                if t >= XR:
                    dve.wait_ge(exp_causal, t - XR + 1)
                cut, done = (t % TB) * P, set()
                for n, (a, b) in enumerate(pieces(t)):
                    h = a // HALF
                    if h not in done:
                        done.add(h)
                        dve.wait_ge(half_filled[h], t + 1)
                    ins = v.tensor_scalar(scores[:, t % XR, a:b], score_bank[h][:, a - h * HALF:b - h * HALF], 0.0,
                                          None, ALU.add, ALU.max, accum_out=maxes[:, t, 1 + n:2 + n])
                    if b in (HALF, S):
                        ins.then_inc(half_drained[h], 1)
                if t >= XR:
                    dve.wait_ge(exp_comp, t - XR + 1)
                dve.wait_ge(comp_filled, t + 1)
                v.tensor_scalar(comp[:, t % XR, :], comp_bank[:, 0:SC], -1.0 / COMP, None, ALU.mult, ALU.min,
                                accum_out=nmax[:, t, 1:2]).then_inc(comp_drained, 1)

            def ffn_weights():
                dve.wait_ge(ffn_w_loaded, 48)
                for src, dst in ((wi_gate[:, :, :], wf_gate[:, :, :]), (wi_up[:, :, :], wf_up[:, :, :]),
                                 (wi_down[:, :], wf_down[:, :])):
                    v.tensor_scalar(dst, src, DEQUANT, None, ALU.mult).then_inc(w_float, 1)
                for n, dst in enumerate((wT_gate[:, :], wT_up[:, :], wT_down[:, :, :].rearrange("p h d -> p (h d)"))):
                    await_fill(dve, "wT", n)
                    v.tensor_scalar(dst, bank("wT", n)[:, 0:H], 0.5 if n == 2 else 1.0, None,
                                    ALU.mult).then_inc(drain_sem("wT", n), 1)

            def ffn(c, h):
                n = c * NH + h
                dve.wait_ge(tanh_ready, n + 1)
                await_fill(dve, "gate", c, h)
                if n >= 1:
                    await_drain(dve, "up", (n - 1) // NH, (n - 1) % NH)
                v.scalar_tensor_tensor(out=gated[:, :], in0=tanh_g[:, n % 2, :], scalar=1.0,
                                       in1=bank("gate", c, h)[:, :], op0=ALU.add,
                                       op1=ALU.mult).then_inc(drain_sem("gate", c, h), 1)
                if c >= 2 and h == 0:
                    await_fill(dve, "down", c - 2)
                await_fill(dve, "up", c, h)
                await_drain(dve, "gate", c, h)
                v.tensor_tensor(hid[:, c % 2, h, :], bank("up", c, h)[:, :], gated[:, :],
                                ALU.mult).then_inc(drain_sem("up", c, h), 1)

            def down(c):
                ts = slice(c * CT, (c + 1) * CT)
                await_fill(dve, "down", c)
                dve.wait_ge(xb_ready, c + 1)
                v.tensor_tensor(base[:, ts, :], bank("down", c)[:, :].rearrange("p (j d) -> p j d", d=D),
                                base[:, ts, :], ALU.add).then_inc(drain_sem("down", c), 1)

            def choose_side(p):
                ts = slice(2 * p, 2 * p + 2)
                dve.wait_ge(counted[2], 2 * p + 2)
                dve.wait_ge(thr_ready[2], 2 * p + 2)
                chain(v.tensor_scalar(d_off[:, ts], signs[:, 2, ts], 0.5, MID, ALU.mult, ALU.add))
                chain(v.tensor_scalar(side[:, ts], d_off[:, ts], 0.0, 2.0, ALU.is_gt, ALU.mult))
                chain(v.tensor_scalar(side[:, ts], side[:, ts], -1.0, None, ALU.add))
                v.tensor_tensor(dist[:, ts], d_off[:, ts], side[:, ts], ALU.mult)
                chain(v.tensor_scalar(nside[:, ts], side[:, ts], -TINY, None, ALU.mult))
                v.scalar_tensor_tensor(out=pick[:, ts], in0=side[:, ts], scalar=0.0, in1=dist[:, ts], op0=ALU.is_gt,
                                       op1=ALU.add)
                chain(v.scalar_tensor_tensor(out=m9[:, ts, 0], in0=nthr[:, 2, ts], scalar=-1.0, in1=nside[:, ts],
                                             op0=ALU.mult, op1=ALU.mult))

            def neighbours(t):
                chain(v.tensor_scalar(sg[:, t % 4, :], sg[:, t % 4, :], side[:, t:t + 1], None, ALU.mult))
                chain(v.scalar_tensor_tensor(out=near[:, :], in0=scores[:, t % XR, :], scalar=nside[:, t:t + 1],
                                             in1=sg[:, t % 4, :], op0=ALU.mult, op1=ALU.min,
                                             accum_out=far[:, t:t + 1]))
                v.max(m9[:, t, 1:9], near[:, :]).then_inc(near_max, 1)
                dve.wait_ge(near_max, t + 1)

            def choose(p):
                ts = slice(2 * p, 2 * p + 2)
                v.tensor_tensor(hot[:, :, :], ramp[:, :, :], pick[:, ts].unsqueeze(2).to_broadcast([P, 2, 9]),
                                ALU.is_equal)
                v.tensor_tensor(hot8[:, :, :], ramp[:, :, 0:8], dist[:, ts].unsqueeze(2).to_broadcast([P, 2, 8]),
                                ALU.is_equal)
                chain(v.tensor_tensor(tied[:, ts], side[:, ts], signs[:, 2, ts], ALU.mult))
                v.tensor_tensor(hot[:, :, :], hot[:, :, :], m9[:, ts, :], ALU.mult)
                v.tensor_tensor(gaps[:, :, :], m9[:, ts, 0:8], m9[:, ts, 1:9], ALU.subtract)
                chain(v.scalar_tensor_tensor(out=tied[:, ts], in0=far[:, ts], scalar=2.0, in1=tied[:, ts],
                                             op0=ALU.mult, op1=ALU.subtract))
                v.tensor_reduce(tau[:, ts], hot[:, :, :], AX_X, ALU.add)
                v.tensor_scalar(tied[:, ts], tied[:, ts], -float(S), None, ALU.is_equal)
                chain(v.tensor_tensor(hot8[:, :, :], hot8[:, :, :], gaps[:, :, :], ALU.mult))
                v.scalar_tensor_tensor(out=tau[:, ts], in0=side[:, ts], scalar=-1.0 / TINY, in1=tau[:, ts],
                                       op0=ALU.mult, op1=ALU.mult)
                chain(v.tensor_reduce(gap[:, ts], hot8[:, :, :], AX_X, ALU.add))
                v.scalar_tensor_tensor(out=good[:, ts], in0=gap[:, ts], scalar=0.0, in1=tied[:, ts], op0=ALU.is_gt,
                                       op1=ALU.mult).then_inc(good_ready, 1)
                await_fill(dve, "check", p)
                v.tensor_reduce(n_good[0:1, p:p + 1], bank("check", p)[0:1, 0:2], AX_X,
                                ALU.add).then_inc(drain_sem("check", p), 1)
                dve.wait_ge(drain_sem("check", p), jobs["check", p][1])
                v.tensor_copy(n_good_i[0:1, p:p + 1], n_good[0:1, p:p + 1]).then_inc(check_read, 1)
                dve.wait_ge(check_read, p + 1)

            def sparse(p):
                if p >= 2:
                    await_fill(dve, "turn", 2 * p - 3, 2)
                sure = dve.value_load(n_good_i[0:1, p:p + 1])
                with dve.If(sure == 2 * P):
                    for t in (2 * p, 2 * p + 1):
                        v.scalar_tensor_tensor(out=p_sparse[:, t % 4, :], in0=scores[:, t % XR, :],
                                               scalar=tau[:, t:t + 1], in1=scores[:, t % XR, :], op0=ALU.is_ge,
                                               op1=ALU.mult).then_inc(sparse_ready, 1)
                with dve.Else():
                    for t in (2 * p, 2 * p + 1):
                        dve.drain()
                        v.tensor_copy(taken[:, :], scores[:, t % XR, :])
                        for r in range(TOP_K // 8):
                            dve.drain()
                            v.max(m9[:, t, 0:8], taken[:, :])
                            dve.drain()
                            v.match_replace(taken[:, :], m9[:, t, 0:8], taken[:, :], LOWEST)
                        dve.drain()
                        v.tensor_tensor(taken[:, :], taken[:, :], scores[:, t % XR, :], ALU.not_equal)
                        dve.drain()
                        v.tensor_tensor(p_sparse[:, t % 4, :], taken[:, :], scores[:, t % XR, :],
                                        ALU.mult).then_inc(sparse_ready, 1)
                for t in (2 * p, 2 * p + 1):
                    n_causal = sum(b <= (t % TB) * P for a, b in pieces(t))
                    w = causal_width(t)
                    diag = scores[:, t % XR, w - P:w]
                    dve.wait_ge(sparse_ready, t + 1)
                    if t == 0:
                        dve.wait_ge(ident_ready, 2)
                    chain(v.tensor_tensor_reduce(out=diag, in0=diag, in1=causal[:, :], scale=1.0, scalar=MASKED,
                                                 op0=ALU.add, op1=ALU.max, accum_out=maxes[:, t, 0:1]))
                    v.tensor_reduce(nmax[:, t, 0:1], maxes[:, t, 0:1 + n_causal], AX_X, ALU.max, negate=True)
                    v.tensor_reduce(nmax[:, t, 2:3], maxes[:, t, 1:5], AX_X, ALU.max,
                                    negate=True).then_inc(nmax_ready, 1)

            def mix(t):
                dve.wait_ge(exp_sparse, t + 1)
                dve.wait_ge(exp_causal, t + 1)
                dve.wait_ge(exp_comp, t + 1)
                v.reciprocal(zinv[:, t, :], zsum[:, t, :]).then_inc(zinv_ready, 1)

            def turn(t):
                if t >= 2:
                    await_fill(dve, "attend", t - 2)
                await_fill(dve, "turn", t, 1)
                v.tensor_copy(pT[:, t % 2, CT * P:2 * CT * P],
                              bank("turn", t, 1)[:, :]).then_inc(drain_sem("turn", t, 1), 1)

            def finish(t):
                await_fill(dve, "attend", t)
                dve.wait_ge(zinv_ready, t + 1)
                await_drain(dve, "down", t // CT)
                v.scalar_tensor_tensor(out=base[:, t, :], in0=bank("attend", t)[:, 0:D],
                                       scalar=zinv[:, t, 2:3], in1=base[:, t, :], op0=ALU.mult,
                                       op1=ALU.add).then_inc(drain_sem("attend", t), 1)

            own = {"consts": consts, "ln": ln, "Q": Q, "kbar": kbar_, "moment": moment, "guess": guess,
                   "comp_k": comp_k, "comp_v": comp_v, "raw": raw, "ffn_weights": ffn_weights, "ffn": ffn,
                   "down": down, "choose_side": choose_side, "neighbours": neighbours, "choose": choose,
                   "sparse": sparse, "mix": mix, "turn": turn, "finish": finish}
            for stage, *a in schedule:
                if stage in own:
                    own[stage](*a)


_INS = ["L0_attn_x", "L0_attn_Wq", "L0_attn_bq", "L0_attn_Wk", "L0_attn_bk", "L0_attn_Wv", "L0_attn_bv",
        "L0_attn_Wo", "L0_attn_bo", "L0_ffn_w_gate", "L0_ffn_w_up", "L0_ffn_w_down"]


def kernel(**inputs):
    import numpy as np
    import concourse.bacc as bacc
    from concourse.bass_utils import run_bass_kernel_spmd

    nc = bacc.Bacc("TRN2", target_bir_lowering=False, num_devices=1)
    arrays, args = {}, []
    for name in _INS:
        a = np.ascontiguousarray(inputs[name])
        arrays[f"{name}_dram"] = a
        args.append(nc.dram_tensor(f"{name}_dram", a.shape, mybir.dt.from_np(a.dtype), kind="ExternalInput").ap())
    shape = arrays["L0_attn_x_dram"].shape
    out = nc.dram_tensor("out_dram", shape, F32, kind="ExternalOutput").ap()
    attention_ffn_block(nc, *args, out)
    r = run_bass_kernel_spmd(nc, [arrays], core_ids=[0])
    return r.results[0]["out_dram"]
```

```python
from contextlib import ExitStack
from math import erf, exp, pi, sqrt

import concourse.bass as bass
from concourse import mybir

ALU = mybir.AluOpType
ACT = mybir.ActivationFunctionType
F32 = mybir.dt.float32
BF16 = mybir.dt.bfloat16
I32 = mybir.dt.int32
AX_X = mybir.AxisListType.X

P = 128
TOP_K = 64
COMP = 4
EPS = 1e-5
TINY = 2.0 ** -60
MASKED = -3.0e38
LOWEST = -3.4e38


TENSOR_ORDER = """
xnT,0@4 K,0@3 xnT,1@2 ffn_weights@431 moment,0,0@2 Q,0@0 moment,0,1@2 K,1@1 moment,0,2@2 Q,1@4 cq,0@0
raw,0 muvar,0@2 raw,1 cq,1@0 raw,2 raw,3 raw,4 muvar,1@2 ffn,0,0@41 raw,5 ffn,0,1@01 V,0@4 V,1@2 vo,0@4
xnT,2@3 xnT,3@1 raw,6 K,2@3 ffn,0,2@14 ffn,1,0@03 check,0@2 Q,2@1 moment,1,0@4 moment,1,1@4 K,3@0 raw,7
down,0@2 ffn,1,1@30 check,1@0 moment,1,2@3 vo,1@4 ffn,1,2@12 cq,2@0 raw,8 muvar,2@0 V,2@3 raw,9
turn,0@143 Q,3@2 ffn,2,0@04 ffn,2,1@30 down,1@4 vco,0@1 raw,10 raw,11 attend,0@1 turn,1@244 check,2@1
turn,2@034 ffn,2,2@03 attend,1@1 turn,3@441 check,3@3 ffn,3,0@20 V,3@3 raw,12 attend,2@4 cq,3@3 muvar,3@3
vo,2@2 turn,4@020 ffn,3,1@21 attend,3@3 raw,13 raw,14 check,4@0 turn,5@430 vo,3@4 attend,4@2 ffn,3,2@04
attend,5@3 raw,15 turn,6@240 turn,7@043 vco,1@3 attend,6@1 attend,7@3 check,5@0 turn,8@401 down,2@2
attend,8@4 down,3@1 check,6@0 turn,9@204 attend,9@0 turn,10@243 turn,11@432 attend,10@4 check,7@3
turn,12@032 attend,11@0 turn,13@234 attend,12@0 attend,13@4 turn,14@043 attend,14@1 turn,15@013
attend,15@2
"""
SCALAR_ORDER = """
xnT,0 K,0 xnT,1 K,1 count,0,0 count,0,1 count,1,0 count,1,1 count,2,0 count,2,1 count,0,2 softmax,0,1
ffn,0,0 count,0,3 count,1,2 count,1,3 ffn,0,1 softmax,1,1 count,2,2 V,0 V,1 count,0,4 count,2,3 vo,0
xnT,2 xnT,3 count,1,4 ffn,0,2 count,0,5 K,2 count,2,4 ffn,1,0 softmax,0,2 softmax,0,0 softmax,2,1 K,3
count,0,6 count,1,5 count,0,7 ffn,1,1 softmax,1,0 count,2,5 softmax,1,2 count,1,6 count,1,7 count,2,6
ffn,1,2 softmax,2,2 vo,1 softmax,3,2 count,2,7 softmax,2,0 V,2 turned,0 softmax,3,1 ffn,2,0 ffn,2,1
softmax,3,0 count,0,8 count,0,9 count,1,8 count,1,9 vco,0 count,0,10 count,1,10 count,2,8 turned,1
turned,2 count,2,9 count,2,10 ffn,2,2 turned,3 softmax,4,0 softmax,4,2 softmax,4,1 softmax,5,2 ffn,3,0
V,3 count,0,11 softmax,5,0 softmax,6,0 count,1,11 softmax,5,1 softmax,6,1 softmax,6,2 vo,2 turned,4
count,2,11 softmax,7,0 ffn,3,1 softmax,7,2 softmax,7,1 count,0,12 count,0,13 turned,5 count,1,12 vo,3
count,1,13 count,0,14 count,1,14 softmax,8,1 ffn,3,2 softmax,8,0 count,2,12 softmax,8,2 count,2,13
turned,6 turned,7 count,2,14 vco,1 softmax,9,2 softmax,9,1 count,0,15 softmax,9,0 turned,8 softmax,10,1
softmax,11,1 softmax,10,0 softmax,10,2 softmax,11,2 count,1,15 softmax,11,0 turned,9 count,2,15
softmax,12,0 softmax,12,1 turned,10 softmax,12,2 turned,11 softmax,13,1 softmax,13,0 softmax,13,2
softmax,14,1 turned,12 softmax,14,2 softmax,14,0 softmax,15,0 softmax,15,1 turned,13 softmax,15,2
turned,14 turned,15
"""
VECTOR_ORDER = """
consts ln_stats,0 ln_stats,1 ln_apply,0 ln_apply,1 ffn_weights ln_stats,2 ln_stats,3 moment,0,0 comp_k,0
moment,0,1 Q,0 moment,0,2 comp_k,1 ln_apply,2 cq,0 kbar,0 evac,0 muvar,0 Q,1 ln_apply,3 evac,1 evac,2
cq,1 evac,3 evac,4 near,0 hidden,0,0 muvar,1 evac,5 hidden,0,1 pick,0 near,1 hidden,0,2 comp_k,2
verdict,0 evac,6 hidden,1,0 moment,1,0 sparse,0 pick,1 evac,7 sparse,1 moment,1,1 sums,0 comp_v,0
hidden,1,1 Q,2 moment,1,2 comp_k,3 down_add,0 verdict,1 kbar,1 sparse,2 sums,1 cq,2 sparse,3 evac,8
hidden,1,2 muvar,2 near,2 comp_v,1 sums,2 hidden,2,0 evac,9 Q,3 pick,2 evac,10 down_add,1 near,3 finish,0
sums,3 hidden,2,1 verdict,2 pick,3 sparse,4 finish,1 hidden,2,2 sparse,5 verdict,3 evac,11 sparse,6
sums,4 hidden,3,0 sparse,7 cq,3 comp_v,2 comp_v,3 evac,12 near,4 muvar,3 sums,5 pick,4 finish,2 sums,6
evac,13 hidden,3,1 finish,3 verdict,4 evac,14 sparse,8 sums,7 near,5 sparse,9 hidden,3,2 finish,4 sums,8
finish,5 evac,15 pick,5 near,6 verdict,5 finish,6 sums,9 finish,7 sparse,10 sparse,11 pick,6 down_add,2
sums,10 verdict,6 finish,8 sums,11 sparse,12 sparse,13 near,7 sums,12 pick,7 finish,9 sums,13 verdict,7
sparse,14 sparse,15 finish,10 sums,14 finish,11 down_add,3 sums,15 finish,12 finish,13 finish,14
finish,15
"""
GPSIMD_ORDER = """
consts ln_stats,0 ln_stats,1 xb,0 ln_stats,2 ln_stats,3 xb,1 xb,2 muvar,0 count,0,0 count,0,1 count,1,0
count,1,1 xb,3 count,0,2 count,0,3 count,1,2 count,1,3 muvar,1 count,0,4 count,0,5 count,1,4 count,0,6
count,0,7 count,1,5 count,1,6 count,1,7 mix,0 muvar,2 mix,1 mix,2 count,0,8 count,0,9 count,1,8
count,0,10 count,1,9 count,1,10 mix,3 mix,4 count,0,11 count,1,11 muvar,3 mix,5 count,0,12 count,0,13
mix,6 count,1,12 count,1,13 count,0,14 mix,7 mix,8 count,1,14 count,0,15 mix,9 count,1,15 mix,10 mix,11
mix,12 mix,13 mix,14 mix,15
"""


def parse(text):
    order, banks = [], {}
    for word in text.split():
        name, _, where = word.partition("@")
        stage, *index = name.split(",")
        key = (stage, *(int(i) for i in index))
        order.append(key)
        banks[key] = [int(b) for b in where]
    return order, banks


def normal_quantile(share):
    low, high = -8.0, 8.0
    for _ in range(60):
        z = (low + high) / 2
        low, high = (z, high) if 0.5 * (1 + erf(z / sqrt(2))) < share else (low, z)
    return z


def attention_ffn_block(nc, x, wq, bq, wk, bk, wv, bv, wo, bo, w_gate, w_up, w_down, out):
    B, S, D = x.shape
    H = w_gate.shape[0]
    NT = B * S // P
    TB = S // P
    CT = 4
    NC = NT // CT
    CB = TB // CT
    CW = CT * P
    NH = H // P
    SC = S // COMP
    CC = SC // P
    HALF = S // 2
    SCALE = 1.0 / sqrt(D)
    DEQUANT = 1.0 / 127.0
    assert D == P and HALF == 512 and CT * P == 512 and S % 512 == 0

    z_top = normal_quantile(1.0 - TOP_K / S)
    per_count = sqrt(2 * pi) * exp(z_top * z_top / 2) / S
    STEPS = (1.0, 0.5)
    MID = S / 2 - TOP_K

    with ExitStack() as ctx:
        def sb(name, shape, dt=F32):
            return ctx.enter_context(nc.sbuf_tensor(name, shape, dt))

        def sem(name):
            return ctx.enter_context(nc.semaphore(name))

        score_bank = [ctx.enter_context(nc.psum_tensor(f"score{h}", [P, HALF], F32)) for h in range(2)]
        comp_bank = ctx.enter_context(nc.psum_tensor("comp_bank", [P, 512], F32))
        NW = 5
        work_bank = [ctx.enter_context(nc.psum_tensor(f"work{i}", [P, 512], F32)) for i in range(NW)]

        XR = 7
        ident = sb("ident", [P, P])
        causal = sb("causal", [P, P])
        ones = sb("ones", [P, 1])
        ramp = sb("ramp", [P, 2, 9])
        half_pow = sb("half_pow", [P, 2, CT])
        x_in = sb("x_in", [P, NT, D])
        xn = sb("xn", [P, NT, D])
        xnT = sb("xnT", [P, NT * P])
        w_in = sb("w_in", [P, 4, D])
        b_in = sb("b_in", [P, 3])
        bo_rows = sb("bo_rows", [P, D])
        wi_gate = sb("wi_gate", [P, NH, D], I32)
        wi_up = sb("wi_up", [P, NH, D], I32)
        wi_down = sb("wi_down", [P, H], I32)
        wf_gate = sb("wf_gate", [P, NH, D])
        wf_up = sb("wf_up", [P, NH, D])
        wf_down = sb("wf_down", [P, H])
        wT_gate = sb("wT_gate", [P, H])
        wT_up = sb("wT_up", [P, H])
        wT_down = sb("wT_down", [P, NH, D])
        bn = sb("bn", [P, NT, 6])
        mv = sb("mv", [P, NT, 2])
        rstd = sb("rstd", [P, NT])
        ln_tmp = sb("ln_tmp", [P, 3, CT])
        qT = sb("qT", [P, NT * P])
        kT = sb("kT", [P, NT * P])
        vT = sb("vT", [P, NT * P])
        kcT = sb("kcT", [P, B * SC])
        vcT = sb("vcT", [P, B * SC])
        ksum = sb("ksum", [P, NC])
        kbar = sb("kbar", [P, B])
        mom = sb("mom", [P, 3, D])
        qcq = sb("qcq", [P, CW])
        vo = sb("vo", [P, NT, D])
        vco = sb("vco", [P, B * CC, D])
        mu_var = sb("mu_var", [P, NT, 2])
        nslope = sb("nslope", [P, 2, NT])
        nthr = sb("nthr", [P, 3, NT])
        nthr_off = sb("nthr_off", [P, 2, NT])
        thr_tmp = sb("thr_tmp", [P, 2, CT])
        signs = sb("signs", [P, 3, NT])
        scores = sb("scores", [P, XR, S])
        comp = sb("comp", [P, XR, SC])
        sg_skip = sb("sg_skip", [P, 2, S], BF16)
        sg = sb("sg", [P, 4, S], BF16)
        near = sb("near", [P, 2, S])
        m9 = sb("m9", [P, NT, 9])
        far = sb("far", [P, NT])
        d_off = sb("d_off", [P, NT])
        side2 = sb("side2", [P, NT])
        side = sb("side", [P, NT])
        nside = sb("nside", [P, NT])
        dist = sb("dist", [P, NT])
        pick = sb("pick", [P, NT])
        hot = sb("hot", [P, 2, 9])
        hot8 = sb("hot8", [P, 2, 8])
        gaps = sb("gaps", [P, 2, 8])
        hot_m = sb("hot_m", [P, 2, 9])
        hot_g = sb("hot_g", [P, 2, 8])
        tau_m = sb("tau_m", [P, NT])
        tau = sb("tau", [P, NT])
        good = sb("good", [P, NT])
        gap = sb("gap", [P, NT])
        tied = sb("tied", [P, NT])
        tied2 = sb("tied2", [P, NT])
        n_good = sb("n_good", [1, NT // 2])
        n_good_i = sb("n_good_i", [1, NT // 2], I32)
        taken = sb("taken", [P, S])
        maxes = sb("maxes", [P, NT, 5])
        nmax = sb("nmax", [P, NT, 3])
        zsum = sb("zsum", [P, NT, 3])
        zinv = sb("zinv", [P, NT, 3])
        ratio = sb("ratio", [P, NT, 2])
        p_sparse = sb("p_sparse", [P, 4, S])
        p_causal = sb("p_causal", [P, 3, S])
        p_comp = sb("p_comp", [P, 3, SC])
        pT = sb("pT", [P, 2, S + SC])
        tanh_g = sb("tanh_g", [P, 2, CW])
        gated = sb("gated", [P, CW])
        hid = sb("hid", [P, 2, NH, CW])
        base = x_in

        x_loaded = [sem(f"x_loaded{c}") for c in range(NC)]
        w_loaded = sem("w_loaded")
        wvo_loaded = sem("wvo_loaded")
        ffn_w_loaded = sem("ffn_w_loaded")
        bo_loaded = sem("bo_loaded")
        ident_ready = sem("ident_ready")
        pool_step = sem("pool_step")
        const_ready = sem("const_ready")
        vec_step = sem("vec_step")
        stats_ready = sem("stats_ready")
        rstd_ready = sem("rstd_ready")
        xn_ready = sem("xn_ready")
        w_float = sem("w_float")
        filled = [sem(f"work_filled{i}") for i in range(NW)]
        drained = [sem(f"work_drained{i}") for i in range(NW)]
        kc_ready = sem("kc_ready")
        vc_ready = sem("vc_ready")
        kbar_ready = sem("kbar_ready")
        half_filled = [sem(f"half_filled{h}") for h in range(2)]
        half_drained = [sem(f"half_drained{h}") for h in range(2)]
        comp_filled = sem("comp_filled")
        comp_drained = sem("comp_drained")
        thr_ready = [sem(f"thr_ready{r}") for r in range(3)]
        counted = [sem(f"counted{r}") for r in range(3)]
        near_done = sem("near_done")
        pick_ready = sem("pick_ready")
        good_ready = sem("good_ready")
        checked = sem("checked")
        check_read = sem("check_read")
        sparse_ready = sem("sparse_ready")
        nmax_sparse = sem("nmax_sparse")
        nmax_causal = sem("nmax_causal")
        exp_sparse = sem("exp_sparse")
        exp_causal = sem("exp_causal")
        exp_comp = sem("exp_comp")
        zinv_ready = sem("zinv_ready")
        mixed = sem("mixed")
        tanh_ready = sem("tanh_ready")
        xb_ready = sem("xb_ready")
        stored = sem("stored")

        tensor_order, banks_of = parse(TENSOR_ORDER)
        jobs, fills = {}, [0] * NW
        for key in tensor_order:
            stage, *a = key
            if stage == "ffn":
                names = [("gate", *a), ("up", *a)]
            elif stage in ("ffn_weights", "turn"):
                names = [(stage, *a, n) for n in range(3)]
            else:
                names = [key]
            for name, b in zip(names, banks_of[key]):
                fills[b] += 1
                jobs[name] = (b, fills[b])

        def bank(*name):
            return work_bank[jobs[name][0]]

        def acquire(pe, *name):
            b, n = jobs[name]
            if n > 1:
                pe.wait_ge(drained[b], n - 1)

        def fill_sem(*name):
            return filled[jobs[name][0]]

        def drain_sem(*name):
            return drained[jobs[name][0]]

        def await_fill(eng, *name):
            eng.wait_ge(filled[jobs[name][0]], jobs[name][1])

        def await_drain(eng, *name):
            eng.wait_ge(drained[jobs[name][0]], jobs[name][1])

        def causal_width(t):
            return (t % TB + 1) * P

        def pieces(t):
            cut = (t % TB) * P
            ends = sorted({0, cut, HALF, S})
            return [(a, b) for a, b in zip(ends[:-1], ends[1:])]

        x_v = x.rearrange("b (c j p) d -> (b c) p j d", p=P, j=CT)
        out_v = out.rearrange("b (t p) d -> (b t) p d", p=P)
        block = ctx.enter_context(nc.Block())

        @block.sync
        def _(sp):
            for c in range(CB):
                sp.dma_start(x_in[:, c * CT:(c + 1) * CT, :], x_v[c]).then_inc(x_loaded[c], 16)
            for i, w in ((1, wk), (0, wq)):
                sp.dma_start(w_in[:, i, :], w).then_inc(w_loaded, 16)
            for i, b in enumerate((bq, bk, bv)):
                sp.dma_start(b_in[:, i:i + 1], b.unsqueeze(1)).then_inc(w_loaded, 16)
            for i, w in ((2, wv), (3, wo)):
                sp.dma_start(w_in[:, i, :], w).then_inc(wvo_loaded, 16)
            sp.dma_start(wi_gate[:, :, :], w_gate.rearrange("(n p) d -> p n d", p=P)).then_inc(ffn_w_loaded, 16)
            sp.dma_start(wi_up[:, :, :], w_up.rearrange("(n p) d -> p n d", p=P)).then_inc(ffn_w_loaded, 16)
            sp.dma_start(wi_down[:, :], w_down).then_inc(ffn_w_loaded, 16)
            sp.dma_start(bo_rows[:, :], bo.unsqueeze(0).to_broadcast([P, D])).then_inc(bo_loaded, 16)
            for c in range(CB, NC):
                sp.dma_start(x_in[:, c * CT:(c + 1) * CT, :], x_v[c]).then_inc(x_loaded[c], 16)
            for t in range(NT):
                await_drain(sp, "attend", t)
                sp.dma_start(out_v[t], base[:, t, :]).then_inc(stored, 16)
            sp.wait_ge(stored, 16 * NT)

        @block.gpsimd
        def _(pool):
            g = nc.gpsimd
            steps = [0]

            def chain(ins):
                steps[0] += 1
                ins.then_inc(pool_step, 1)
                pool.wait_ge(pool_step, steps[0])

            def consts():
                chain(g.memset(ident[:], 0.0))
                g.affine_select(out=ident[:], in_=ident[:], compare_op=ALU.not_equal, fill=1.0, base=0,
                                pattern=[[-1, P]], channel_multiplier=1).then_inc(ident_ready, 1)
                chain(g.memset(causal[:], 0.0))
                g.affine_select(out=causal[:], in_=causal[:], compare_op=ALU.is_ge, fill=MASKED, base=0,
                                pattern=[[-1, P]], channel_multiplier=1).then_inc(ident_ready, 1)

            def ln(c):
                v, a, r = ln_tmp[:, 0, :], ln_tmp[:, 1, :], ln_tmp[:, 2, :]
                pool.wait_ge(stats_ready, c + 1)
                if c == 0:
                    pool.wait_ge(const_ready, 1)
                chain(g.tensor_scalar(v, mv[:, c * CT:(c + 1) * CT, 1], EPS, None, ALU.add))
                chain(g.tensor_tensor(r, v, half_pow[:, 0, :], ALU.pow))
                chain(g.tensor_tensor(a, r, r, ALU.mult))
                chain(g.tensor_tensor(a, a, v, ALU.mult))
                chain(g.tensor_scalar(a, a, -0.5, 1.5, ALU.mult, ALU.add))
                g.tensor_tensor(rstd[:, c * CT:(c + 1) * CT], r, a, ALU.mult).then_inc(rstd_ready, 1)

            def guess(c):
                ts = slice(c * CT, (c + 1) * CT)
                dev, off = thr_tmp[:, 0, :], thr_tmp[:, 1, :]
                await_drain(pool, "muvar", c)
                chain(g.tensor_scalar(dev, mu_var[:, ts, 1], 1e-30, None, ALU.max))
                chain(g.tensor_tensor(dev, dev, half_pow[:, 1, :], ALU.pow))
                for r in range(2):
                    g.tensor_scalar(nslope[:, r, ts], dev, -per_count * STEPS[r] / 2, None, ALU.mult).then_inc(pool_step, 1)
                    steps[0] += 1
                pool.wait_ge(pool_step, steps[0])
                chain(g.tensor_scalar(dev, dev, -z_top, None, ALU.mult))
                chain(g.tensor_tensor(nthr[:, 0, ts], dev, mu_var[:, ts, 0], ALU.subtract))
                chain(g.tensor_scalar(off, nslope[:, 0, ts], 2 * MID, None, ALU.mult))
                g.tensor_tensor(nthr_off[:, 0, ts], off, nthr[:, 0, ts], ALU.add).then_inc(thr_ready[0], 1)

            def count(r, t):
                col = slice(t, t + 1)
                pool.wait_ge(counted[r], t + 1)
                nxt = g.tensor_scalar(nthr[:, r + 1, col], signs[:, r, col], nslope[:, r, col], nthr_off[:, r, col],
                                      ALU.mult, ALU.add)
                nxt.then_inc(thr_ready[r + 1], 1)
                if r == 0:
                    pool.wait_ge(thr_ready[1], t + 1)
                    chain(g.tensor_scalar(nthr_off[:, 1, col], nslope[:, 1, col], 2 * MID, nthr[:, 1, col],
                                          ALU.mult, ALU.add))

            def mix(t):
                w = causal_width(t)
                pool.wait_ge(zinv_ready, t + 1)
                chain(g.tensor_scalar(ratio[:, t, :], zinv[:, t, 0:2], zsum[:, t, 2:3], 1.0, ALU.mult, ALU.mult))
                pc, pw, ps = p_comp[:, t % 3, :], p_causal[:, t % 3, 0:w], p_sparse[:, t % 4, 0:w]
                g.tensor_scalar(pc, pc, ratio[:, t, 1:2], 1.0, ALU.mult, ALU.mult)
                chain(g.tensor_scalar(pw, pw, ratio[:, t, 0:1], 1.0, ALU.mult, ALU.mult))
                g.tensor_tensor(ps, ps, pw, ALU.add).then_inc(mixed, 1)

            def xb(c):
                ts = slice(c * CT, (c + 1) * CT)
                pool.wait_ge(xn_ready, (c + 1) * CT)
                pool.wait_ge(bo_loaded, 16)
                g.tensor_tensor(base[:, ts, :], x_in[:, ts, :], bo_rows[:, :].unsqueeze(1).to_broadcast([P, CT, D]),
                                ALU.add).then_inc(xb_ready, 1)

            own = {"consts": consts, "ln_stats": ln, "muvar": guess, "count": count, "mix": mix, "xb": xb}
            for stage, *a in parse(GPSIMD_ORDER)[0]:
                own[stage](*a)

        @block.tensor
        def _(pe):
            mm = nc.tensor.matmul

            def turned(dst, src):
                return mm(dst, src, ident[:], start=True, stop=True, is_transpose=True)

            def xnT_(c):
                acquire(pe, "xnT", c)
                if c == 0:
                    pe.wait_ge(ident_ready, 1)
                for j in range(CT):
                    pe.wait_ge(xn_ready, c * CT + j + 1)
                    last = turned(bank("xnT", c)[:, j * P:(j + 1) * P], xn[:, c * CT + j, :])
                last.then_inc(fill_sem("xnT", c), 1)

            def project(name, i, c):
                acquire(pe, name, c)
                pe.wait_ge(*((wvo_loaded, 32) if i == 2 else (w_loaded, 80)))
                await_drain(pe, "xnT", c)
                mm(bank(name, c)[:, :], w_in[:, i, :], xnT[:, c * CW:(c + 1) * CW], start=True,
                   stop=True).then_inc(fill_sem(name, c), 1)

            def moment(b, n):
                acquire(pe, "moment", b, n)
                if n == 0:
                    pe.wait_ge(xn_ready, (b + 1) * TB)
                    for j in range(TB):
                        last = mm(bank("moment", b, 0)[:, 0:D], xn[:, b * TB + j, :], xn[:, b * TB + j, :],
                                  start=(j == 0), stop=(j == TB - 1))
                else:
                    pe.wait_ge(w_loaded, 80)
                    await_drain(pe, "moment", b, n - 1)
                    lhsT, rhs = (mom[:, 0, :], w_in[:, 1, :]) if n == 1 else (w_in[:, 1, :], mom[:, 1, :])
                    last = mm(bank("moment", b, n)[:, 0:D], lhsT, rhs, start=True, stop=True)
                last.then_inc(fill_sem("moment", b, n), 1)

            def cq(c):
                acquire(pe, "cq", c)
                await_drain(pe, "moment", c // CB, 2)
                await_drain(pe, "Q", c)
                mm(bank("cq", c)[:, :], mom[:, 2, :], qT[:, c * CW:(c + 1) * CW], start=True,
                   stop=True).then_inc(fill_sem("cq", c), 1)

            def muvar(c):
                acquire(pe, "muvar", c)
                pe.wait_ge(kbar_ready, c // CB + 1)
                pe.wait_ge(const_ready, 1)
                await_drain(pe, "cq", c)
                for j in range(CT):
                    mm(bank("muvar", c)[:, 2 * j:2 * j + 1], qT[:, c * CW + j * P:c * CW + (j + 1) * P],
                       kbar[:, c // CB:c // CB + 1], start=True, stop=True)
                    last = mm(bank("muvar", c)[:, 2 * j + 1:2 * j + 2], qcq[:, j * P:(j + 1) * P], ones[:, 0:1],
                              start=True, stop=True)
                last.then_inc(fill_sem("muvar", c), 1)

            def raw(t):
                b, q = t // TB, qT[:, t * P:(t + 1) * P]
                await_drain(pe, "Q", t // CT)
                for h in range(2):
                    await_drain(pe, "K", b * CB + h)
                    if t >= 1:
                        pe.wait_ge(half_drained[h], t)
                    mm(score_bank[h][:, :], q, kT[:, b * S + h * HALF:b * S + (h + 1) * HALF], start=True,
                       stop=True).then_inc(half_filled[h], 1)
                if t >= 1:
                    pe.wait_ge(comp_drained, t)
                pe.wait_ge(kc_ready, (b + 1) * CB)
                mm(comp_bank[:, 0:SC], q, kcT[:, b * SC:(b + 1) * SC], start=True, stop=True).then_inc(comp_filled, 1)

            def vo_(c):
                acquire(pe, "vo", c)
                await_drain(pe, "V", c)
                for j in range(CT):
                    last = mm(bank("vo", c)[:, j * D:(j + 1) * D], vT[:, c * CW + j * P:c * CW + (j + 1) * P],
                              w_in[:, 3, :], start=True, stop=True)
                last.then_inc(fill_sem("vo", c), 1)

            def vco_(b):
                acquire(pe, "vco", b)
                pe.wait_ge(vc_ready, (b + 1) * CB)
                for j in range(CC):
                    last = mm(bank("vco", b)[:, j * D:(j + 1) * D], vcT[:, b * SC + j * P:b * SC + (j + 1) * P],
                              w_in[:, 3, :], start=True, stop=True)
                last.then_inc(fill_sem("vco", b), 1)

            def ffn_weights():
                for n, w in enumerate((wf_gate, wf_up, wf_down)):
                    acquire(pe, "ffn_weights", n)
                    pe.wait_ge(w_float, n + 1)
                    for j in range(NH):
                        src = w[:, j * P:(j + 1) * P] if n == 2 else w[:, j, :]
                        last = turned(bank("ffn_weights", n)[:, j * P:(j + 1) * P], src)
                    last.then_inc(fill_sem("ffn_weights", n), 1)

            def ffn(c, h):
                for n in range(2):
                    await_drain(pe, "ffn_weights", n)
                await_drain(pe, "xnT", c)
                for name, w in (("gate", wT_gate), ("up", wT_up)):
                    acquire(pe, name, c, h)
                    mm(bank(name, c, h)[:, :], w[:, h * P:(h + 1) * P], xnT[:, c * CW:(c + 1) * CW], start=True,
                       stop=True).then_inc(fill_sem(name, c, h), 1)

            def down(c):
                acquire(pe, "down", c)
                await_drain(pe, "ffn_weights", 2)
                for h in range(NH):
                    await_drain(pe, "up", c, h)
                for j in range(CT):
                    for h in range(NH):
                        last = mm(bank("down", c)[:, j * D:(j + 1) * D], hid[:, c % 2, h, j * P:(j + 1) * P],
                                  wT_down[:, h, :], start=(h == 0), stop=(h == NH - 1))
                last.then_inc(fill_sem("down", c), 1)

            def check(p):
                acquire(pe, "check", p)
                pe.wait_ge(good_ready, p + 1)
                mm(bank("check", p)[0:1, 0:2], ones[:, 0:1], good[:, 2 * p:2 * p + 2], start=True,
                   stop=True).then_inc(fill_sem("check", p), 1)

            def turn(t):
                pe.wait_ge(mixed, t + 1)
                for n in range(3):
                    acquire(pe, "turn", t, n)
                    for j in range(CC if n == 2 else CT):
                        src = p_comp[:, t % 3, j * P:(j + 1) * P] if n == 2 else \
                            p_sparse[:, t % 4, (n * CT + j) * P:(n * CT + j + 1) * P]
                        last = turned(bank("turn", t, n)[:, j * P:(j + 1) * P], src)
                    last.then_inc(fill_sem("turn", t, n), 1)

            def attend(t):
                b = t // TB
                acquire(pe, "attend", t)
                for c in range(b * CB, (b + 1) * CB):
                    await_drain(pe, "vo", c)
                await_drain(pe, "vco", b)
                for n in range(3):
                    await_drain(pe, "turn", t, n)
                    for j in range(CC if n == 2 else CT):
                        k = n * CT + j
                        v = vco[:, b * CC + j, :] if n == 2 else vo[:, b * TB + k, :]
                        last = mm(bank("attend", t)[:, 0:D], pT[:, t % 2, k * P:(k + 1) * P], v,
                                  start=(k == 0), stop=(k == TB + CC - 1))
                last.then_inc(fill_sem("attend", t), 1)

            own = {"xnT": xnT_, "Q": lambda c: project("Q", 0, c), "K": lambda c: project("K", 1, c),
                   "V": lambda c: project("V", 2, c), "moment": moment, "cq": cq, "muvar": muvar, "raw": raw, "vo": vo_,
                   "vco": vco_, "ffn_weights": ffn_weights, "ffn": ffn, "down": down, "check": check,
                   "turn": turn, "attend": attend}
            for stage, *a in tensor_order:
                own[stage](*a)

        @block.scalar
        def _(act):
            a_ = nc.scalar.activation

            def xnT_(c):
                await_fill(act, "xnT", c)
                a_(xnT[:, c * CW:(c + 1) * CW], bank("xnT", c)[:, :], ACT.Copy).then_inc(drain_sem("xnT", c), 1)

            def K(c):
                await_fill(act, "K", c)
                act.wait_ge(w_loaded, 16 * 5)
                a_(kT[:, c * CW:(c + 1) * CW], bank("K", c)[:, :], ACT.Identity, bias=b_in[:, 1:2],
                   accum_out=ksum[:, c:c + 1]).then_inc(drain_sem("K", c), 1)

            def V(c):
                await_fill(act, "V", c)
                act.wait_ge(w_loaded, 16 * 5)
                a_(vT[:, c * CW:(c + 1) * CW], bank("V", c)[:, :], ACT.Identity,
                   bias=b_in[:, 2:3]).then_inc(drain_sem("V", c), 1)

            def vo_(c):
                await_fill(act, "vo", c)
                a_(vo[:, c * CT:(c + 1) * CT, :], bank("vo", c)[:, :].rearrange("p (j d) -> p j d", d=D), ACT.Copy,
                   scale=1.0 / 3.0).then_inc(drain_sem("vo", c), 1)

            def vco_(b):
                await_fill(act, "vco", b)
                a_(vco[:, b * CC:(b + 1) * CC, :], bank("vco", b)[:, 0:CC * D].rearrange("p (j d) -> p j d", d=D),
                   ACT.Copy, scale=1.0 / (3.0 * COMP)).then_inc(drain_sem("vco", b), 1)

            def count(r, t):
                if r == 0:
                    act.wait_ge(half_drained[0], t + 1)
                    act.wait_ge(half_drained[1], t + 1)
                    act.wait_ge(thr_ready[0], t // CT + 1)
                else:
                    act.wait_ge(thr_ready[r], t + 1)
                if r == 2 and t >= 4:
                    act.wait_ge(near_done, t - 3)
                dst = sg[:, t % 4, :] if r == 2 else sg_skip[:, r, :]
                if r < 2 and t:
                    act.wait_ge(counted[r], t)
                a_(dst, scores[:, t % XR, :], ACT.Sign, bias=nthr[:, r, t:t + 1], scale=1.0,
                   accum_out=signs[:, r, t:t + 1]).then_inc(counted[r], 1)

            def softmax(t, which):
                w = causal_width(t)
                if which == 2:
                    act.wait_ge(sparse_ready, t + 1)
                    act.wait_ge(nmax_sparse, t + 1)
                    a_(p_sparse[:, t % 4, :], p_sparse[:, t % 4, :], ACT.Exp, bias=nmax[:, t, 2:3],
                       accum_out=zsum[:, t, 2:3]).then_inc(exp_sparse, 1)
                    return
                if t >= 3:
                    await_fill(act, "turn", t - 3, 2)
                if which == 0:
                    act.wait_ge(nmax_causal, t + 1)
                    a_(p_causal[:, t % 3, 0:w], scores[:, t % XR, 0:w], ACT.Exp, bias=nmax[:, t, 0:1],
                       accum_out=zsum[:, t, 0:1]).then_inc(exp_causal, 1)
                else:
                    act.wait_ge(comp_drained, t + 1)
                    a_(p_comp[:, t % 3, :], comp[:, t % XR, :], ACT.Exp, bias=nmax[:, t, 1:2], scale=-1.0,
                       accum_out=zsum[:, t, 1:2]).then_inc(exp_comp, 1)

            def turned(t):
                if t >= 2:
                    await_fill(act, "attend", t - 2)
                for n in range(3):
                    await_fill(act, "turn", t, n)
                    w = CC * P if n == 2 else CT * P
                    a_(pT[:, t % 2, n * CT * P:n * CT * P + w], bank("turn", t, n)[:, 0:w],
                       ACT.Copy).then_inc(drain_sem("turn", t, n), 1)

            def ffn(c, h):
                n = c * NH + h
                await_fill(act, "gate", c, h)
                if n >= 2:
                    await_drain(act, "gate", (n - 2) // NH, (n - 2) % NH)
                a_(tanh_g[:, n % 2, :], bank("gate", c, h)[:, :], ACT.Tanh, scale=0.5).then_inc(tanh_ready, 1)

            own = {"xnT": xnT_, "K": K, "V": V, "vo": vo_, "vco": vco_, "count": count, "softmax": softmax,
                   "turned": turned, "ffn": ffn}
            for stage, *a in parse(SCALAR_ORDER)[0]:
                own[stage](*a)

        @block.vector
        def _(dve):
            v = nc.vector
            steps = [0]
            sure = {}

            def mark(ins):
                steps[0] += 1
                ins.then_inc(vec_step, 1)
                return steps[0]

            def chain(ins):
                dve.wait_ge(vec_step, mark(ins))

            def consts():
                v.memset(half_pow[:, 0, :], -0.5)
                v.memset(half_pow[:, 1, :], 0.5)
                v.memset(maxes[:, :, :], 0.0)
                for j in range(9):
                    v.memset(ramp[:, :, j:j + 1], float(j))
                v.memset(ones[:, :], 1.0).then_inc(const_ready, 1)
                dve.wait_ge(const_ready, 1)

            def ln_stats(c):
                dve.wait_ge(x_loaded[c], 16)
                for t in range(c * CT, (c + 1) * CT):
                    last = v.bn_stats(bn[:, t, :], x_in[:, t, :])
                chain(last)
                for t in range(c * CT, (c + 1) * CT):
                    last = v.bn_aggr(mv[:, t, :], bn[:, t, :])
                last.then_inc(stats_ready, 1)

            def ln_apply(c):
                dve.wait_ge(rstd_ready, c + 1)
                for t in range(c * CT, (c + 1) * CT):
                    v.tensor_scalar(xn[:, t, :], x_in[:, t, :], mv[:, t, 0:1], rstd[:, t:t + 1], ALU.subtract,
                                    ALU.mult).then_inc(xn_ready, 1)

            def Q(c):
                await_fill(dve, "Q", c)
                dve.wait_ge(w_loaded, 16 * 5)
                v.tensor_scalar(qT[:, c * CW:(c + 1) * CW], bank("Q", c)[:, :], b_in[:, 0:1], SCALE, ALU.add,
                                ALU.mult).then_inc(drain_sem("Q", c), 1)

            def kbar_(b):
                for c in range(b * CB, (b + 1) * CB):
                    await_drain(dve, "K", c)
                chain(v.tensor_reduce(kbar[:, b:b + 1], ksum[:, b * CB:(b + 1) * CB], AX_X, ALU.add))
                v.tensor_scalar(kbar[:, b:b + 1], kbar[:, b:b + 1], 1.0 / S, None, ALU.mult).then_inc(kbar_ready, 1)

            def moment(b, n):
                await_fill(dve, "moment", b, n)
                if n == 2 and b:
                    await_fill(dve, "cq", b * CB - 1)
                v.tensor_scalar(mom[:, n, :], bank("moment", b, n)[:, 0:D], 1.0 / S if n == 0 else 1.0, None,
                                ALU.mult).then_inc(drain_sem("moment", b, n), 1)

            def cq(c):
                await_fill(dve, "cq", c)
                if c >= 1:
                    await_fill(dve, "muvar", c - 1)
                v.tensor_tensor(qcq[:, :], bank("cq", c)[:, :], qT[:, c * CW:(c + 1) * CW],
                                ALU.mult).then_inc(drain_sem("cq", c), 1)

            def muvar(c):
                await_fill(dve, "muvar", c)
                v.tensor_copy(mu_var[:, c * CT:(c + 1) * CT, :],
                              bank("muvar", c)[:, 0:2 * CT].rearrange("p (j s) -> p j s", s=2)
                              ).then_inc(drain_sem("muvar", c), 1)

            def comp_k(c):
                await_drain(dve, "K", c)
                v.tensor_reduce(kcT[:, c * P:(c + 1) * P],
                                kT[:, c * CW:(c + 1) * CW].rearrange("p (n r) -> p n r", r=COMP), AX_X,
                                ALU.add).then_inc(kc_ready, 1)

            def comp_v(c):
                await_drain(dve, "V", c)
                v.tensor_reduce(vcT[:, c * P:(c + 1) * P],
                                vT[:, c * CW:(c + 1) * CW].rearrange("p (n r) -> p n r", r=COMP), AX_X,
                                ALU.add).then_inc(vc_ready, 1)

            def evac(t):
                if t >= XR:
                    dve.wait_ge(exp_causal, t - XR + 1)
                cut, done = (t % TB) * P, set()
                for n, (a, b) in enumerate(pieces(t)):
                    h = a // HALF
                    if h not in done:
                        done.add(h)
                        dve.wait_ge(half_filled[h], t + 1)
                    ins = v.tensor_scalar(scores[:, t % XR, a:b], score_bank[h][:, a - h * HALF:b - h * HALF], 0.0,
                                          None, ALU.add, ALU.max, accum_out=maxes[:, t, 1 + n:2 + n])
                    if b in (HALF, S):
                        ins.then_inc(half_drained[h], 1)
                if t >= XR:
                    dve.wait_ge(exp_comp, t - XR + 1)
                dve.wait_ge(comp_filled, t + 1)
                v.tensor_scalar(comp[:, t % XR, :], comp_bank[:, 0:SC], -1.0 / COMP, None, ALU.mult, ALU.min,
                                accum_out=nmax[:, t, 1:2]).then_inc(comp_drained, 1)

            def ffn_weights():
                dve.wait_ge(ffn_w_loaded, 48)
                for src, dst in ((wi_gate[:, :, :], wf_gate[:, :, :]), (wi_up[:, :, :], wf_up[:, :, :]),
                                 (wi_down[:, :], wf_down[:, :])):
                    v.tensor_scalar(dst, src, DEQUANT, None, ALU.mult).then_inc(w_float, 1)
                for n, dst in enumerate((wT_gate[:, :], wT_up[:, :], wT_down[:, :, :].rearrange("p h d -> p (h d)"))):
                    await_fill(dve, "ffn_weights", n)
                    v.tensor_scalar(dst, bank("ffn_weights", n)[:, 0:H], 0.5 if n == 2 else 1.0, None,
                                    ALU.mult).then_inc(drain_sem("ffn_weights", n), 1)

            def hidden(c, h):
                n = c * NH + h
                await_fill(dve, "gate", c, h)
                dve.wait_ge(tanh_ready, n + 1)
                if n:
                    await_drain(dve, "up", (n - 1) // NH, (n - 1) % NH)
                v.scalar_tensor_tensor(out=gated[:, :], in0=tanh_g[:, n % 2, :], scalar=1.0,
                                       in1=bank("gate", c, h)[:, :], op0=ALU.add,
                                       op1=ALU.mult).then_inc(drain_sem("gate", c, h), 1)
                if c >= 2 and h == 0:
                    await_fill(dve, "down", c - 2)
                await_fill(dve, "up", c, h)
                await_drain(dve, "gate", c, h)
                v.tensor_tensor(hid[:, c % 2, h, :], bank("up", c, h)[:, :], gated[:, :],
                                ALU.mult).then_inc(drain_sem("up", c, h), 1)

            def down_add(c):
                ts = slice(c * CT, (c + 1) * CT)
                await_fill(dve, "down", c)
                dve.wait_ge(xb_ready, c + 1)
                v.tensor_tensor(base[:, ts, :], bank("down", c)[:, :].rearrange("p (j d) -> p j d", d=D),
                                base[:, ts, :], ALU.add).then_inc(drain_sem("down", c), 1)

            def near_(p):
                ts = slice(2 * p, 2 * p + 2)
                dve.wait_ge(counted[2], 2 * p + 2)
                dve.wait_ge(thr_ready[2], 2 * p + 2)
                v.tensor_scalar(d_off[:, ts], signs[:, 2, ts], 0.5, MID, ALU.mult, ALU.add)
                chain(v.tensor_scalar(side2[:, ts], signs[:, 2, ts], -2 * MID, 2.0, ALU.is_gt, ALU.mult))
                v.tensor_scalar(nside[:, ts], side2[:, ts], -TINY, TINY, ALU.mult, ALU.add)
                chain(v.tensor_scalar(side[:, ts], side2[:, ts], -1.0, None, ALU.add))
                flipped = [mark(v.tensor_scalar(sg[:, t % 4, :], sg[:, t % 4, :], side[:, t:t + 1], None, ALU.mult))
                           for t in (2 * p, 2 * p + 1)]
                v.tensor_tensor(dist[:, ts], d_off[:, ts], side[:, ts], ALU.mult)
                v.tensor_tensor(tied[:, ts], side[:, ts], signs[:, 2, ts], ALU.mult)
                small = mark(v.scalar_tensor_tensor(out=m9[:, ts, 0], in0=nthr[:, 2, ts], scalar=-1.0,
                                                    in1=nside[:, ts], op0=ALU.mult, op1=ALU.mult))
                for t in (2 * p, 2 * p + 1):
                    dve.wait_ge(vec_step, flipped[t % 2])
                    v.scalar_tensor_tensor(out=near[:, t % 2, :], in0=scores[:, t % XR, :],
                                           scalar=nside[:, t:t + 1], in1=sg[:, t % 4, :], op0=ALU.mult,
                                           op1=ALU.min, accum_out=far[:, t:t + 1]).then_inc(near_done, 1)
                dve.wait_ge(vec_step, small)
                v.scalar_tensor_tensor(out=pick[:, ts], in0=side2[:, ts], scalar=0.5, in1=dist[:, ts],
                                       op0=ALU.mult, op1=ALU.add).then_inc(pick_ready, 1)

            def pick_(p):
                ts = slice(2 * p, 2 * p + 2)
                dve.wait_ge(near_done, 2 * p + 1)
                v.max(m9[:, 2 * p, 1:9], near[:, 0, :])
                dve.wait_ge(near_done, 2 * p + 2)
                found = mark(v.max(m9[:, 2 * p + 1, 1:9], near[:, 1, :]))
                dve.wait_ge(pick_ready, p + 1)
                v.tensor_tensor(hot[:, :, :], ramp[:, :, :], pick[:, ts].unsqueeze(2).to_broadcast([P, 2, 9]),
                                ALU.is_equal)
                v.tensor_tensor(hot8[:, :, :], ramp[:, :, 0:8], dist[:, ts].unsqueeze(2).to_broadcast([P, 2, 8]),
                                ALU.is_equal)
                first = mark(v.scalar_tensor_tensor(out=tied2[:, ts], in0=far[:, ts], scalar=2.0, in1=tied[:, ts],
                                                    op0=ALU.mult, op1=ALU.subtract))
                dve.wait_ge(vec_step, found)
                v.tensor_tensor(gaps[:, :, :], m9[:, ts, 0:8], m9[:, ts, 1:9], ALU.subtract)
                dve.wait_ge(vec_step, first)
                v.tensor_tensor(hot_m[:, :, :], hot[:, :, :], m9[:, ts, :], ALU.mult)
                chain(v.tensor_scalar(tied[:, ts], tied2[:, ts], -float(S), None, ALU.is_equal))
                v.tensor_tensor(hot_g[:, :, :], hot8[:, :, :], gaps[:, :, :], ALU.mult)
                chain(v.tensor_reduce(tau_m[:, ts], hot_m[:, :, :], AX_X, ALU.add))
                v.tensor_reduce(gap[:, ts], hot_g[:, :, :], AX_X, ALU.add)
                chain(v.scalar_tensor_tensor(out=tau[:, ts], in0=side[:, ts], scalar=-1.0 / TINY, in1=tau_m[:, ts],
                                             op0=ALU.mult, op1=ALU.mult))
                v.scalar_tensor_tensor(out=good[:, ts], in0=gap[:, ts], scalar=0.0, in1=tied[:, ts], op0=ALU.is_gt,
                                       op1=ALU.mult).then_inc(good_ready, 1)

            def verdict(p):
                await_fill(dve, "check", p)
                v.tensor_reduce(n_good[0:1, p:p + 1], bank("check", p)[0:1, 0:2], AX_X,
                                ALU.add).then_inc(drain_sem("check", p), 1)
                await_drain(dve, "check", p)
                v.tensor_copy(n_good_i[0:1, p:p + 1], n_good[0:1, p:p + 1]).then_inc(check_read, 1)

            def sparse(t):
                if t >= 4:
                    await_fill(dve, "turn", t - 4, 2)
                row, dst = scores[:, t % XR, :], p_sparse[:, t % 4, :]
                if t % 2 == 0:
                    dve.wait_ge(check_read, t // 2 + 1)
                    sure[t // 2] = dve.value_load(n_good_i[0:1, t // 2:t // 2 + 1])
                with dve.If(sure[t // 2] == 2 * P):
                    v.scalar_tensor_tensor(out=dst, in0=row, scalar=tau[:, t:t + 1], in1=row, op0=ALU.is_ge,
                                           op1=ALU.mult).then_inc(sparse_ready, 1)
                with dve.Else():
                    dve.drain()
                    v.tensor_copy(taken[:, :], row)
                    for r in range(TOP_K // 8):
                        dve.drain()
                        v.max(m9[:, t, 0:8], taken[:, :])
                        dve.drain()
                        v.match_replace(taken[:, :], m9[:, t, 0:8], taken[:, :], LOWEST)
                    dve.drain()
                    v.tensor_tensor(taken[:, :], taken[:, :], row, ALU.not_equal)
                    dve.drain()
                    v.tensor_tensor(dst, taken[:, :], row, ALU.mult).then_inc(sparse_ready, 1)
                n_causal = sum(b <= (t % TB) * P for a, b in pieces(t))
                w = causal_width(t)
                diag = scores[:, t % XR, w - P:w]
                dve.wait_ge(sparse_ready, t + 1)
                if t == 0:
                    dve.wait_ge(ident_ready, 2)
                v.tensor_reduce(nmax[:, t, 2:3], maxes[:, t, 1:5], AX_X, ALU.max,
                                negate=True).then_inc(nmax_sparse, 1)
                chain(v.tensor_tensor_reduce(out=diag, in0=diag, in1=causal[:, :], scale=1.0, scalar=MASKED,
                                             op0=ALU.add, op1=ALU.max, accum_out=maxes[:, t, 0:1]))
                v.tensor_reduce(nmax[:, t, 0:1], maxes[:, t, 0:1 + n_causal], AX_X, ALU.max,
                                negate=True).then_inc(nmax_causal, 1)

            def sums(t):
                dve.wait_ge(exp_sparse, t + 1)
                dve.wait_ge(exp_causal, t + 1)
                dve.wait_ge(exp_comp, t + 1)
                v.reciprocal(zinv[:, t, :], zsum[:, t, :]).then_inc(zinv_ready, 1)

            def finish(t):
                await_fill(dve, "attend", t)
                dve.wait_ge(zinv_ready, t + 1)
                await_drain(dve, "down", t // CT)
                v.scalar_tensor_tensor(out=base[:, t, :], in0=bank("attend", t)[:, 0:D],
                                       scalar=zinv[:, t, 2:3], in1=base[:, t, :], op0=ALU.mult,
                                       op1=ALU.add).then_inc(drain_sem("attend", t), 1)

            own = {"consts": consts, "ln_stats": ln_stats, "ln_apply": ln_apply, "Q": Q, "kbar": kbar_,
                   "moment": moment, "cq": cq, "muvar": muvar, "comp_k": comp_k, "comp_v": comp_v, "evac": evac,
                   "ffn_weights": ffn_weights, "hidden": hidden, "down_add": down_add,
                   "near": near_, "pick": pick_, "verdict": verdict,
                   "sparse": sparse, "sums": sums, "finish": finish}
            for stage, *a in parse(VECTOR_ORDER)[0]:
                own[stage](*a)


_INS = ["L0_attn_x", "L0_attn_Wq", "L0_attn_bq", "L0_attn_Wk", "L0_attn_bk", "L0_attn_Wv", "L0_attn_bv",
        "L0_attn_Wo", "L0_attn_bo", "L0_ffn_w_gate", "L0_ffn_w_up", "L0_ffn_w_down"]


def kernel(**inputs):
    import numpy as np
    import concourse.bacc as bacc
    from concourse.bass_utils import run_bass_kernel_spmd

    nc = bacc.Bacc("TRN2", target_bir_lowering=False, num_devices=1)
    arrays, args = {}, []
    for name in _INS:
        a = np.ascontiguousarray(inputs[name])
        arrays[f"{name}_dram"] = a
        args.append(nc.dram_tensor(f"{name}_dram", a.shape, mybir.dt.from_np(a.dtype), kind="ExternalInput").ap())
    shape = arrays["L0_attn_x_dram"].shape
    out = nc.dram_tensor("out_dram", shape, F32, kind="ExternalOutput").ap()
    attention_ffn_block(nc, *args, out)
    r = run_bass_kernel_spmd(nc, [arrays], core_ids=[0])
    return r.results[0]["out_dram"]
```

```python
from contextlib import ExitStack
from math import erf, exp, pi, sqrt

import concourse.bass as bass
from concourse import mybir

ALU = mybir.AluOpType
ACT = mybir.ActivationFunctionType
F32 = mybir.dt.float32
BF16 = mybir.dt.bfloat16
I32 = mybir.dt.int32
AX_X = mybir.AxisListType.X

P = 128
TOP_K = 64
COMP = 4
EPS = 1e-5
TINY = 2.0 ** -60
MASKED = -3.0e38
LOWEST = -3.4e38


TENSOR_ORDER = """
warm_up xnT,0@1 K,0@1 xnT,1@0 V,0@2 K,1@0 Q,0@2 moment,0,0@4 Q,1@1 moment,0,1@0 V,1@3 moment,0,2@2 raw,0
cq,0@2 vo,0@1 muvar,0@3 raw,1 raw,2 raw,3 raw,4 cq,1@4 raw,5 muvar,1@4 xnT,2@1 xnT,3@2 K,2@1 K,3@4
ffn_weights,0@2 ffn_weights,1@0 V,2@3 raw,6 up,0,0@2 check,0@4 up,0,1@1 raw,7 V,3@4 Q,3@0 gate,0,0@2
Q,2@3 gate,0,1@4 vo,1@0 moment,1,0@3 ffn_weights,2@2 raw,8 moment,1,1@1 turn,0,1@2 turn,0,2@0 check,1@1
gate,0,2@4 moment,1,2@2 up,0,2@3 up,1,0@2 cq,3@1 raw,9 turn,1,1@3 gate,1,0@0 muvar,3@4 up,1,1@1
turn,0,0@4 turn,1,0@2 vo,2@1 raw,10 down,0@4 vco,0@3 check,2@2 cq,2@3 turn,1,2@2 attend,0@0 turn,2,2@1
gate,1,1@4 raw,11 gate,1,2@2 attend,1@1 muvar,2@0 gate,3,0@3 up,1,2@1 turn,2,1@4 turn,2,0@1 turn,3,0@0
raw,12 up,3,0@4 check,3@1 turn,3,1@0 turn,3,2@1 turn,4,2@2 gate,3,1@4 attend,2@3 raw,13 up,3,1@0
turn,4,1@0 attend,3@1 turn,4,0@4 turn,5,0@2 down,1@3 turn,5,1@4 raw,14 check,4@3 turn,5,2@1 attend,4@0
turn,6,2@3 turn,6,1@2 turn,6,0@1 attend,5@4 gate,3,2@1 up,3,2@3 raw,15 turn,7,2@2 attend,6@0 up,2,0@1
gate,2,0@4 gate,2,1@2 turn,7,1@3 vo,3@0 turn,7,0@1 up,2,1@4 up,2,2@3 vco,1@1 check,5@0 turn,8,0@3
gate,2,2@1 turn,8,1@0 attend,7@4 turn,8,2@3 turn,9,2@2 down,3@1 turn,9,0@0 turn,9,1@2 check,6@3 down,2@4
turn,10,2@3 attend,8@1 turn,10,0@2 turn,10,1@0 turn,11,2@4 attend,9@1 turn,11,1@3 turn,11,0@2 attend,10@0
turn,12,2@3 turn,12,1@4 turn,13,1@2 turn,12,0@3 check,7@4 attend,11@1 attend,12@3 turn,13,0@0 turn,13,2@1
turn,14,1@4 turn,15,1@3 turn,14,2@0 attend,13@1 turn,14,0@4 turn,15,2@0 turn,15,0@1 attend,14@3
attend,15@4
"""
SCALAR_ORDER = """
xnT,0 K,0 xnT,1 V,0 K,1 Q,0 Q,1 V,1 softmax,0,1 vo,0 count,0,0 count,0,1 count,1,0 count,0,2 count,1,1
count,2,0 count,2,1 count,1,2 xnT,2 xnT,3 count,0,3 K,2 K,3 count,0,4 count,1,3 ffn_weights,0
ffn_weights,1 count,0,5 count,1,4 count,0,6 count,2,2 count,2,3 up,0,0 V,2 up,0,1 V,3 softmax,0,0
softmax,1,0 Q,3 Q,2 gate,0,0 softmax,0,2 gate,0,1 softmax,1,1 softmax,1,2 count,1,5 ffn_weights,2 vo,1
count,1,6 turned,0,1 count,0,7 softmax,2,1 count,2,4 up,0,2 gate,0,2 count,2,5 turned,0,2 softmax,2,0
softmax,2,2 up,1,0 softmax,3,0 up,1,1 softmax,3,1 turned,0,0 turned,1,0 turned,1,1 softmax,3,2 count,1,7
count,0,8 gate,1,0 count,0,9 vco,0 vo,2 count,2,6 count,0,10 count,1,8 turned,1,2 turned,2,2 count,2,7
softmax,4,1 softmax,5,1 softmax,4,2 softmax,4,0 count,1,9 gate,1,1 gate,1,2 softmax,5,2 up,1,2 count,0,11
turned,2,1 turned,2,0 turned,3,0 softmax,5,0 gate,3,0 count,1,10 up,3,0 count,2,8 count,2,9 gate,3,1
turned,3,1 count,0,12 count,1,11 softmax,6,2 up,3,1 turned,3,2 turned,4,2 softmax,6,0 softmax,6,1
turned,4,1 softmax,7,1 count,2,10 turned,4,0 count,0,13 turned,5,0 softmax,7,0 count,2,11 turned,5,1
softmax,7,2 count,1,12 softmax,8,1 turned,5,2 count,1,13 count,0,14 turned,6,0 turned,6,2 turned,6,1
softmax,8,2 gate,3,2 softmax,8,0 up,3,2 count,2,12 turned,7,2 softmax,9,1 softmax,9,2 count,2,13 up,2,0
gate,2,0 count,0,15 softmax,9,0 turned,7,1 turned,7,0 vo,3 up,2,1 up,2,2 vco,1 gate,2,1 count,1,14
softmax,10,1 turned,8,0 gate,2,2 count,1,15 softmax,10,2 turned,8,2 turned,8,1 turned,9,2 softmax,10,0
softmax,11,2 turned,9,0 softmax,11,1 softmax,12,1 turned,9,1 softmax,11,0 count,2,14 count,2,15
softmax,12,2 turned,10,2 turned,10,0 softmax,13,1 turned,10,1 softmax,12,0 softmax,13,0 turned,11,1
turned,11,2 softmax,13,2 turned,11,0 turned,12,2 turned,12,1 softmax,14,1 softmax,15,1 turned,12,0
softmax,14,2 softmax,15,2 softmax,14,0 softmax,15,0 turned,13,0 turned,13,2 turned,13,1 turned,14,1
turned,14,2 turned,15,1 turned,14,0 turned,15,0 turned,15,2
"""
VECTOR_ORDER = """
consts ln_stats,0 ln_stats,1 ln_apply,0 ln_apply,1 ln_stats,2 ln_stats,3 moment,0,0 kbar,0 moment,0,1
moment,0,2 evac,0 cq,0 muvar,0 ln_apply,2 evac,1 evac,2 evac,3 ln_apply,3 evac,4 cq,1 evac,5 muvar,1
near,0 pick,0 kbar,1 evac,6 verdict,0 sparse,0 mask,0 mask,1 near,1 evac,7 hidden,0,0 sums,0 moment,1,0
pick,1 moment,1,1 hidden,0,1 evac,8 moment,1,2 verdict,1 sums,1 sparse,1 mask,2 cq,3 hidden,0,2 mask,3
evac,9 sums,2 muvar,3 near,2 sums,3 pick,2 hidden,1,0 verdict,2 evac,10 down_add,0 cq,2 sparse,2 finish,0
mask,4 near,3 finish,1 sums,4 evac,11 hidden,1,1 muvar,2 hidden,1,2 mask,5 pick,3 hidden,3,0 verdict,3
sums,5 evac,12 sparse,3 hidden,3,1 finish,2 mask,6 mask,7 near,4 sums,6 evac,13 finish,3 pick,4
down_add,1 evac,14 verdict,4 sums,7 sparse,4 mask,8 near,5 finish,4 mask,9 finish,5 evac,15 sums,8
hidden,3,2 pick,5 finish,6 hidden,2,0 near,6 verdict,5 sums,9 sparse,5 hidden,2,1 hidden,2,2 mask,10
pick,6 finish,7 sums,10 down_add,3 verdict,6 mask,11 sparse,6 down_add,2 sums,11 mask,12 mask,13 finish,8
near,7 sums,12 pick,7 finish,9 sums,13 verdict,7 sparse,7 finish,10 finish,11 mask,14 mask,15 sums,14
finish,12 sums,15 finish,13 finish,14 finish,15
"""
GPSIMD_ORDER = """
consts ln_stats,0 ln_stats,1 xn16,0 xn16,1 comp_k,0 q_bias comp_k,1 q16,0 ln_stats,2 muvar,0 ln_stats,3
count,0,0 count,0,1 q16,1 count,1,0 count,0,2 count,1,1 comp_v,0 dequant,0 dequant,1 dequant,2 muvar,1
count,0,3 comp_v,1 count,0,4 comp_k,2 comp_k,3 count,0,5 count,1,2 count,0,6 count,1,3 count,1,4 xn16,2
xn16,3 comp_v,2 comp_v,3 q16,3 ratios,0 hidden,0,0 count,1,5 xb,0 xb,1 hidden,0,1 count,0,7 ratios,1
mix,0 mix,1 hidden,0,2 count,1,6 muvar,3 q16,2 count,1,7 ratios,2 ratios,3 count,0,8 count,0,9 hidden,1,0
mix,2 count,0,10 xb,2 mix,3 ratios,4 mix,4 hidden,1,1 count,0,11 hidden,1,2 count,1,8 count,1,9 muvar,2
ratios,5 count,0,12 count,1,10 count,1,11 mix,5 xb,3 ratios,6 count,0,13 mix,6 hidden,3,0 hidden,3,1
count,1,12 count,1,13 count,0,14 ratios,7 mix,7 ratios,8 hidden,3,2 mix,8 hidden,2,0 count,0,15 ratios,9
mix,9 count,1,14 count,1,15 hidden,2,1 hidden,2,2 ratios,10 mix,10 ratios,11 mix,11 ratios,12 mix,12
ratios,13 mix,13 ratios,14 ratios,15 mix,14 mix,15
"""


def parse(text):
    order, banks = [], {}
    for word in text.split():
        name, _, where = word.partition("@")
        stage, *index = name.split(",")
        key = (stage, *(int(i) for i in index))
        order.append(key)
        banks[key] = [int(b) for b in where]
    return order, banks


def normal_quantile(share):
    low, high = -8.0, 8.0
    for _ in range(60):
        z = (low + high) / 2
        low, high = (z, high) if 0.5 * (1 + erf(z / sqrt(2))) < share else (low, z)
    return z


def attention_ffn_block(nc, x, wq, bq, wk, bk, wv, bv, wo, bo, w_gate, w_up, w_down, out):
    B, S, D = x.shape
    H = w_gate.shape[0]
    NT = B * S // P
    TB = S // P
    CT = 4
    NC = NT // CT
    CB = TB // CT
    CW = CT * P
    NH = H // P
    SC = S // COMP
    CC = SC // P
    WARM_UP = 13
    HALF = S // 2
    SCALE = 1.0 / sqrt(D)
    DEQUANT = 1.0 / 127.0
    assert D == P and HALF == 512 and CT * P == 512 and S % 512 == 0

    z_top = normal_quantile(1.0 - TOP_K / S)
    per_count = sqrt(2 * pi) * exp(z_top * z_top / 2) / S
    STEPS = (1.0, 0.5)
    MID = S / 2 - TOP_K

    with ExitStack() as ctx:
        def sb(name, shape, dt=F32):
            return ctx.enter_context(nc.sbuf_tensor(name, shape, dt))

        def sem(name):
            return ctx.enter_context(nc.semaphore(name))

        score_bank = [ctx.enter_context(nc.psum_tensor(f"score{h}", [P, HALF], F32)) for h in range(2)]
        comp_bank = ctx.enter_context(nc.psum_tensor("comp_bank", [P, 512], F32))
        NW = 5
        work_bank = [ctx.enter_context(nc.psum_tensor(f"work{i}", [P, 512], F32)) for i in range(NW)]

        XR = 7
        CR = 7
        ident = sb("ident", [P, P])
        causal = sb("causal", [P, P])
        ones = sb("ones", [P, 1])
        ramp = sb("ramp", [P, 2, 2, 9])
        half_pow = sb("half_pow", [P, 2, CT])
        x_in = sb("x_in", [P, NT, D])
        xn = sb("xn", [P, NT, D])
        xnT = sb("xnT", [P, NT * P])
        w_in = sb("w_in", [P, 4, D])
        b_in = sb("b_in", [P, 3])
        q_bias = sb("q_bias", [P, 1])
        bo_rows = sb("bo_rows", [P, D])
        wi_gate = sb("wi_gate", [P, NH, D], I32)
        wi_up = sb("wi_up", [P, NH, D], I32)
        wi_down = sb("wi_down", [P, H], I32)
        wf_gate = sb("wf_gate", [P, NH, D])
        wf_up = sb("wf_up", [P, NH, D])
        wf_down = sb("wf_down", [P, H])
        wT_gate = sb("wT_gate", [P, H])
        wT_up = sb("wT_up", [P, H])
        wT_down = sb("wT_down", [P, NH, D])
        bn = sb("bn", [P, NT, 6])
        mv = sb("mv", [P, NT, 2])
        rstd = sb("rstd", [P, NT])
        ln_tmp = sb("ln_tmp", [P, 3, CT])
        qT = sb("qT", [P, NT * P])
        kT = sb("kT", [P, NT * P])
        vT = sb("vT", [P, NT * P])
        kcT = sb("kcT", [P, B * SC])
        vcT = sb("vcT", [P, B * SC])
        ksum = sb("ksum", [P, NC])
        kbar_sum = sb("kbar_sum", [P, B])
        kbar = sb("kbar", [P, B], BF16)
        xn16 = sb("xn16", [P, TB, D], BF16)
        wk16 = sb("wk16", [P, D], BF16)
        q16 = sb("q16", [P, CW], BF16)
        ones16 = sb("ones16", [P, 1], BF16)
        mom = sb("mom", [P, 2, D], BF16)
        qcq = sb("qcq", [P, CW], BF16)
        vo = sb("vo", [P, NT, D])
        vco = sb("vco", [P, B * CC, D])
        mu_var = sb("mu_var", [P, NT, 2])
        nslope = sb("nslope", [P, 2, NT])
        nthr = sb("nthr", [P, 3, NT])
        nthr_off = sb("nthr_off", [P, 2, NT])
        thr_tmp = sb("thr_tmp", [P, 2, CT])
        signs = sb("signs", [P, 3, NT])
        scores = sb("scores", [P, XR, S])
        comp = sb("comp", [P, CR, SC])
        sg_skip = sb("sg_skip", [P, 2, S], BF16)
        sg = sb("sg", [P, 4, S], BF16)
        near = sb("near", [P, 2, S])
        m9 = sb("m9", [P, NT, 2, 9])
        far = sb("far", [P, NT])
        d_off = sb("d_off", [P, NT])
        side2 = sb("side2", [P, NT])
        side = sb("side", [P, NT])
        nside = sb("nside", [P, NT])
        sel = sb("sel", [P, NT, 2])
        hot = sb("hot", [P, 2, 2, 9])
        hot_m = sb("hot_m", [P, 2, 2, 9])
        picked = sb("picked", [P, NT, 2])
        tau = sb("tau", [P, NT])
        good = sb("good", [P, NT])
        tied = sb("tied", [P, NT])
        tied2 = sb("tied2", [P, NT])
        n_good_i = sb("n_good_i", [1, NT // 2], I32)
        maxes = sb("maxes", [P, NT, 5])
        nmax = sb("nmax", [P, NT, 3])
        zsum = sb("zsum", [P, NT, 3])
        zinv = sb("zinv", [P, NT, 3])
        ratio = sb("ratio", [P, NT, 2])
        p_sparse = sb("p_sparse", [P, 4, S])
        p_causal = sb("p_causal", [P, 3, S])
        p_comp = sb("p_comp", [P, 3, SC])
        pT = sb("pT", [P, 2, S + SC])
        tanh_g = sb("tanh_g", [P, 2, CW])
        up_sb = sb("up_sb", [P, 2, CW])
        comp_tmp = sb("comp_tmp", [P, P, 2])
        hid = sb("hid", [P, 2, NH, CW])
        base = x_in

        x_loaded = [sem(f"x_loaded{c}") for c in range(NC)]
        w_loaded = sem("w_loaded")
        wvo_loaded = sem("wvo_loaded")
        ffn_w_loaded = sem("ffn_w_loaded")
        bo_loaded = sem("bo_loaded")
        ident_ready = sem("ident_ready")
        pool_step = sem("pool_step")
        const_ready = sem("const_ready")
        vec_step = sem("vec_step")
        stats_ready = sem("stats_ready")
        rstd_ready = sem("rstd_ready")
        xn_ready = sem("xn_ready")
        w_float = sem("w_float")
        filled = [sem(f"work_filled{i}") for i in range(NW)]
        drained = [sem(f"work_drained{i}") for i in range(NW)]
        qbias_ready = sem("qbias_ready")
        wk16_ready = sem("wk16_ready")
        xn16_ready = sem("xn16_ready")
        q16_ready = sem("q16_ready")
        hid_ready = sem("hid_ready")
        kc_ready = sem("kc_ready")
        vc_ready = sem("vc_ready")
        kbar_ready = sem("kbar_ready")
        half_filled = [sem(f"half_filled{h}") for h in range(2)]
        half_drained = [sem(f"half_drained{h}") for h in range(2)]
        comp_filled = sem("comp_filled")
        comp_drained = sem("comp_drained")
        thr_ready = [sem(f"thr_ready{r}") for r in range(3)]
        counted = [sem(f"counted{r}") for r in range(3)]
        near_done = sem("near_done")
        pick_ready = sem("pick_ready")
        good_ready = sem("good_ready")
        sparse_ready = sem("sparse_ready")
        nmax_sparse = sem("nmax_sparse")
        nmax_causal = sem("nmax_causal")
        exp_sparse = sem("exp_sparse")
        exp_causal = sem("exp_causal")
        exp_comp = sem("exp_comp")
        zinv_ready = sem("zinv_ready")
        comp_scaled = sem("comp_scaled")
        mixed = sem("mixed")
        tanh_ready = sem("tanh_ready")
        xb_ready = sem("xb_ready")
        stored = sem("stored")

        def row_tile(t):
            p = t // 2 if t < NT - TB else (2 * NT - TB) // 2 - 1 - t // 2
            return 2 * p + t % 2

        CHUNKS = list(dict.fromkeys(row_tile(t) // CT for t in range(NT)))
        CHUNK_BEFORE = dict(zip(CHUNKS[1:], CHUNKS[:-1]))

        tensor_order, banks_of = parse(TENSOR_ORDER)
        jobs, fills = {}, [0] * NW
        for key in tensor_order:
            stage, *a = key
            for b in banks_of[key]:
                fills[b] += 1
                jobs[key] = (b, fills[b])

        def bank(*name):
            return work_bank[jobs[name][0]]

        def acquire(pe, *name):
            b, n = jobs[name]
            if n > 1:
                pe.wait_ge(drained[b], n - 1)

        def fill_sem(*name):
            return filled[jobs[name][0]]

        def drain_sem(*name):
            return drained[jobs[name][0]]

        def await_fill(eng, *name):
            eng.wait_ge(filled[jobs[name][0]], jobs[name][1])

        def await_drain(eng, *name):
            eng.wait_ge(drained[jobs[name][0]], jobs[name][1])

        def causal_width(t):
            return (row_tile(t) % TB + 1) * P

        def pieces(t):
            cut = row_tile(t) % TB * P
            ends = sorted({0, cut, HALF, S})
            return [(a, b) for a, b in zip(ends[:-1], ends[1:])]

        x_v = x.rearrange("b (c j p) d -> (b c) p j d", p=P, j=CT)
        out_v = out.rearrange("b (t p) d -> (b t) p d", p=P)
        block = ctx.enter_context(nc.Block())

        @block.sync
        def _(sp):
            for c in range(CB):
                sp.dma_start(x_in[:, c * CT:(c + 1) * CT, :], x_v[c]).then_inc(x_loaded[c], 16)
            for i, w in ((1, wk), (0, wq)):
                sp.dma_start(w_in[:, i, :], w).then_inc(w_loaded, 16)
            for i, b in enumerate((bq, bk, bv)):
                sp.dma_start(b_in[:, i:i + 1], b.unsqueeze(1)).then_inc(w_loaded, 16)
            for i, w in ((2, wv), (3, wo)):
                sp.dma_start(w_in[:, i, :], w).then_inc(wvo_loaded, 16)
            sp.dma_start(wi_gate[:, :, :], w_gate.rearrange("(n p) d -> p n d", p=P)).then_inc(ffn_w_loaded, 16)
            sp.dma_start(wi_up[:, :, :], w_up.rearrange("(n p) d -> p n d", p=P)).then_inc(ffn_w_loaded, 16)
            sp.dma_start(wi_down[:, :], w_down).then_inc(ffn_w_loaded, 16)
            sp.dma_start(bo_rows[:, :], bo.unsqueeze(0).to_broadcast([P, D])).then_inc(bo_loaded, 16)
            for c in range(CB, NC):
                sp.dma_start(x_in[:, c * CT:(c + 1) * CT, :], x_v[c]).then_inc(x_loaded[c], 16)
            for t in range(NT):
                await_drain(sp, "attend", t)
                r = row_tile(t)
                sp.dma_start(out_v[r], base[:, r, :]).then_inc(stored, 16)
            sp.wait_ge(stored, 16 * NT)

        @block.gpsimd
        def _(pool):
            g = nc.gpsimd
            steps = [0]

            def chain(ins):
                steps[0] += 1
                ins.then_inc(pool_step, 1)
                pool.wait_ge(pool_step, steps[0])

            def consts():
                chain(g.memset(ident[:], 0.0))
                g.affine_select(out=ident[:], in_=ident[:], compare_op=ALU.not_equal, fill=1.0, base=0,
                                pattern=[[-1, P]], channel_multiplier=1).then_inc(ident_ready, 1)
                chain(g.memset(causal[:], 0.0))
                g.affine_select(out=causal[:], in_=causal[:], compare_op=ALU.is_ge, fill=MASKED, base=0,
                                pattern=[[-1, P]], channel_multiplier=1).then_inc(ident_ready, 1)

            def q_bias_():
                pool.wait_ge(w_loaded, 16 * 5)
                g.tensor_scalar(q_bias[:, :], b_in[:, 0:1], SCALE, 1.0, ALU.mult, ALU.mult).then_inc(qbias_ready, 1)
                g.tensor_copy(wk16[:, :], w_in[:, 1, :]).then_inc(wk16_ready, 1)

            def xn16_(c):
                pool.wait_ge(xn_ready, (c + 1) * CT)
                if c >= CB:
                    await_fill(pool, "moment", c // CB - 1, 0)
                g.tensor_copy(xn16[:, c % CB * CT:(c % CB + 1) * CT, :],
                              xn[:, c * CT:(c + 1) * CT, :]).then_inc(xn16_ready, 1)

            def q16_(c):
                await_drain(pool, "Q", c)
                if c:
                    await_fill(pool, "muvar", CHUNK_BEFORE[c])
                g.tensor_copy(q16[:, :], qT[:, c * CW:(c + 1) * CW]).then_inc(q16_ready, 1)

            def ln(c):
                v, a, r = ln_tmp[:, 0, :], ln_tmp[:, 1, :], ln_tmp[:, 2, :]
                pool.wait_ge(stats_ready, c + 1)
                if c == 0:
                    pool.wait_ge(const_ready, 1)
                chain(g.tensor_scalar(v, mv[:, c * CT:(c + 1) * CT, 1], EPS, None, ALU.add))
                chain(g.tensor_tensor(r, v, half_pow[:, 0, :], ALU.pow))
                chain(g.tensor_tensor(a, r, r, ALU.mult))
                chain(g.tensor_tensor(a, a, v, ALU.mult))
                chain(g.tensor_scalar(a, a, -0.5, 1.5, ALU.mult, ALU.add))
                g.tensor_tensor(rstd[:, c * CT:(c + 1) * CT], r, a, ALU.mult).then_inc(rstd_ready, 1)

            def guess(c):
                ts = slice(c * CT, (c + 1) * CT)
                dev, off = thr_tmp[:, 0, :], thr_tmp[:, 1, :]
                await_drain(pool, "muvar", c)
                chain(g.tensor_scalar(dev, mu_var[:, ts, 1], 1e-30, None, ALU.max))
                chain(g.tensor_tensor(dev, dev, half_pow[:, 1, :], ALU.pow))
                for r in range(2):
                    g.tensor_scalar(nslope[:, r, ts], dev, -per_count * STEPS[r] / 2, None,
                                    ALU.mult).then_inc(pool_step, 1)
                    steps[0] += 1
                pool.wait_ge(pool_step, steps[0])
                chain(g.tensor_scalar(dev, dev, -z_top, None, ALU.mult))
                chain(g.tensor_tensor(nthr[:, 0, ts], dev, mu_var[:, ts, 0], ALU.subtract))
                chain(g.tensor_scalar(off, nslope[:, 0, ts], 2 * MID, None, ALU.mult))
                g.tensor_tensor(nthr_off[:, 0, ts], off, nthr[:, 0, ts], ALU.add).then_inc(thr_ready[0], 1)

            def count(r, t):
                col = slice(row_tile(t), row_tile(t) + 1)
                pool.wait_ge(counted[r], t + 1)
                nxt = g.tensor_scalar(nthr[:, r + 1, col], signs[:, r, col], nslope[:, r, col], nthr_off[:, r, col],
                                      ALU.mult, ALU.add)
                nxt.then_inc(thr_ready[r + 1], 1)
                if r == 0:
                    pool.wait_ge(thr_ready[1], t + 1)
                    chain(g.tensor_scalar(nthr_off[:, 1, col], nslope[:, 1, col], 2 * MID, nthr[:, 1, col],
                                          ALU.mult, ALU.add))

            def ratios(t):
                r = row_tile(t)
                pool.wait_ge(zinv_ready, t + 1)
                chain(g.tensor_scalar(ratio[:, r, :], zinv[:, r, 0:2], zsum[:, r, 2:3], 1.0, ALU.mult, ALU.mult))
                pc = p_comp[:, t % 3, :]
                g.tensor_scalar(pc, pc, ratio[:, r, 1:2], 1.0, ALU.mult, ALU.mult).then_inc(comp_scaled, 1)

            def mix(t):
                r = row_tile(t)
                w = causal_width(t)
                pw, ps = p_causal[:, t % 3, 0:w], p_sparse[:, t % 4, 0:w]
                pool.wait_ge(comp_scaled, t + 1)
                chain(g.tensor_scalar(pw, pw, ratio[:, r, 0:1], 1.0, ALU.mult, ALU.mult))
                g.tensor_tensor(ps, ps, pw, ALU.add).then_inc(mixed, 1)

            def compress(src, dst, c, ready):
                quads = src[:, c * CW:(c + 1) * CW].rearrange("p (n r) -> p n r", r=COMP)
                chain(g.tensor_tensor(comp_tmp[:, :, :], quads[:, :, 0:2], quads[:, :, 2:4], ALU.add))
                g.tensor_tensor(dst[:, c * P:(c + 1) * P], comp_tmp[:, :, 0], comp_tmp[:, :, 1],
                                ALU.add).then_inc(ready, 1)
                pool.wait_ge(ready, c + 1)

            def comp_k(c):
                await_drain(pool, "K", c)
                compress(kT, kcT, c, kc_ready)

            def comp_v(c):
                await_drain(pool, "V", c)
                compress(vT, vcT, c, vc_ready)

            def dequant(n):
                pool.wait_ge(ffn_w_loaded, 48)
                src, dst = ((wi_gate, wf_gate), (wi_up, wf_up), (wi_down, wf_down))[n]
                g.tensor_scalar(dst[:], src[:], DEQUANT, 1.0, ALU.mult, ALU.mult).then_inc(w_float, 1)

            def hidden(c, h):
                n = CHUNKS.index(c) * NH + h
                await_drain(pool, "gate", c, h)
                await_drain(pool, "up", c, h)
                if c >= 2 and h == 0:
                    await_fill(pool, "down", c - 2)
                g.tensor_tensor(hid[:, c % 2, h, :], up_sb[:, n % 2, :], tanh_g[:, n % 2, :],
                                ALU.mult).then_inc(hid_ready, 1)

            def xb(c):
                ts = slice(c * CT, (c + 1) * CT)
                pool.wait_ge(xn_ready, (c + 1) * CT)
                pool.wait_ge(bo_loaded, 16)
                g.tensor_tensor(base[:, ts, :], x_in[:, ts, :], bo_rows[:, :].unsqueeze(1).to_broadcast([P, CT, D]),
                                ALU.add).then_inc(xb_ready, 1)

            own = {"consts": consts, "q_bias": q_bias_, "xn16": xn16_, "q16": q16_, "comp_k": comp_k,
                   "comp_v": comp_v, "dequant": dequant, "hidden": hidden, "ln_stats": ln, "muvar": guess,
                   "count": count, "ratios": ratios, "mix": mix, "xb": xb}
            for stage, *a in parse(GPSIMD_ORDER)[0]:
                own[stage](*a)

        @block.tensor
        def _(pe):
            mm = nc.tensor.matmul

            def turned(dst, src):
                return mm(dst, src, ident[:], start=True, stop=True, is_transpose=True)

            def warm_up():
                pe.wait_ge(ident_ready, 1)
                for _ in range(WARM_UP):
                    mm(comp_bank[:, 0:P], ident[:], ident[:], start=True, stop=True)

            def xnT_(c):
                acquire(pe, "xnT", c)
                if c == 0:
                    pe.wait_ge(ident_ready, 1)
                for j in range(CT):
                    pe.wait_ge(xn_ready, c * CT + j + 1)
                    last = turned(bank("xnT", c)[:, j * P:(j + 1) * P], xn[:, c * CT + j, :])
                last.then_inc(fill_sem("xnT", c), 1)

            def project(name, i, c):
                acquire(pe, name, c)
                pe.wait_ge(*((wvo_loaded, 32) if i == 2 else (w_loaded, 80)))
                await_drain(pe, "xnT", c)
                mm(bank(name, c)[:, :], w_in[:, i, :], xnT[:, c * CW:(c + 1) * CW], start=True,
                   stop=True).then_inc(fill_sem(name, c), 1)

            def moment(b, n):
                acquire(pe, "moment", b, n)
                if n == 0:
                    pe.wait_ge(xn16_ready, (b + 1) * CB)
                    for j in range(TB):
                        last = mm(bank("moment", b, 0)[:, 0:D], xn16[:, j, :], xn16[:, j, :],
                                  start=(j == 0), stop=(j == TB - 1))
                else:
                    pe.wait_ge(wk16_ready, 1)
                    await_drain(pe, "moment", b, n - 1)
                    lhsT, rhs = (mom[:, 0, :], wk16[:, :]) if n == 1 else (wk16[:, :], mom[:, 1, :])
                    last = mm(bank("moment", b, n)[:, 0:D], lhsT, rhs, start=True, stop=True)
                last.then_inc(fill_sem("moment", b, n), 1)

            def cq(c):
                acquire(pe, "cq", c)
                await_drain(pe, "moment", c // CB, 2)
                pe.wait_ge(q16_ready, CHUNKS.index(c) + 1)
                mm(bank("cq", c)[:, :], mom[:, 0, :], q16[:, :], start=True,
                   stop=True).then_inc(fill_sem("cq", c), 1)

            def muvar(c):
                acquire(pe, "muvar", c)
                pe.wait_ge(kbar_ready, c // CB + 1)
                pe.wait_ge(const_ready, 1)
                await_drain(pe, "cq", c)
                for j in range(CT):
                    mm(bank("muvar", c)[:, 2 * j:2 * j + 1], q16[:, j * P:(j + 1) * P],
                       kbar[:, c // CB:c // CB + 1], start=True, stop=True)
                    last = mm(bank("muvar", c)[:, 2 * j + 1:2 * j + 2], qcq[:, j * P:(j + 1) * P], ones16[:, 0:1],
                              start=True, stop=True)
                last.then_inc(fill_sem("muvar", c), 1)

            def raw(t):
                r = row_tile(t)
                b, q = t // TB, qT[:, r * P:(r + 1) * P]
                await_drain(pe, "Q", r // CT)
                for h in range(2):
                    await_drain(pe, "K", b * CB + h)
                    if t >= 1:
                        pe.wait_ge(half_drained[h], t)
                    mm(score_bank[h][:, :], q, kT[:, b * S + h * HALF:b * S + (h + 1) * HALF], start=True,
                       stop=True).then_inc(half_filled[h], 1)
                if t >= 1:
                    pe.wait_ge(comp_drained, t)
                pe.wait_ge(kc_ready, (b + 1) * CB)
                mm(comp_bank[:, 0:SC], q, kcT[:, b * SC:(b + 1) * SC], start=True, stop=True).then_inc(comp_filled, 1)

            def vo_(c):
                acquire(pe, "vo", c)
                await_drain(pe, "V", c)
                for j in range(CT):
                    last = mm(bank("vo", c)[:, j * D:(j + 1) * D], vT[:, c * CW + j * P:c * CW + (j + 1) * P],
                              w_in[:, 3, :], start=True, stop=True)
                last.then_inc(fill_sem("vo", c), 1)

            def vco_(b):
                acquire(pe, "vco", b)
                pe.wait_ge(vc_ready, (b + 1) * CB)
                for j in range(CC):
                    last = mm(bank("vco", b)[:, j * D:(j + 1) * D], vcT[:, b * SC + j * P:b * SC + (j + 1) * P],
                              w_in[:, 3, :], start=True, stop=True)
                last.then_inc(fill_sem("vco", b), 1)

            def ffn_weights(n):
                w = (wf_gate, wf_up, wf_down)[n]
                acquire(pe, "ffn_weights", n)
                pe.wait_ge(w_float, n + 1)
                for j in range(NH):
                    src = w[:, j * P:(j + 1) * P] if n == 2 else w[:, j, :]
                    last = turned(bank("ffn_weights", n)[:, j * P:(j + 1) * P], src)
                last.then_inc(fill_sem("ffn_weights", n), 1)

            def ffn(name, n, w, c, h):
                await_drain(pe, "ffn_weights", n)
                await_drain(pe, "xnT", c)
                acquire(pe, name, c, h)
                mm(bank(name, c, h)[:, :], w[:, h * P:(h + 1) * P], xnT[:, c * CW:(c + 1) * CW], start=True,
                   stop=True).then_inc(fill_sem(name, c, h), 1)

            def gate(c, h):
                ffn("gate", 0, wT_gate, c, h)

            def up(c, h):
                ffn("up", 1, wT_up, c, h)

            def down(c):
                acquire(pe, "down", c)
                await_drain(pe, "ffn_weights", 2)
                pe.wait_ge(hid_ready, (CHUNKS.index(c) + 1) * NH)
                for j in range(CT):
                    for h in range(NH):
                        last = mm(bank("down", c)[:, j * D:(j + 1) * D], hid[:, c % 2, h, j * P:(j + 1) * P],
                                  wT_down[:, h, :], start=(h == 0), stop=(h == NH - 1))
                last.then_inc(fill_sem("down", c), 1)

            def check(p):
                acquire(pe, "check", p)
                pe.wait_ge(good_ready, p + 1)
                r = row_tile(2 * p)
                for j in range(2):
                    last = mm(bank("check", p)[0:1, 0:1], ones[:, 0:1], good[:, r + j:r + j + 1], start=(j == 0),
                              stop=(j == 1))
                last.then_inc(fill_sem("check", p), 1)

            def turn(t, n):
                if n == 2:
                    pe.wait_ge(comp_scaled, t + 1)
                elif n * HALF < causal_width(t):
                    pe.wait_ge(mixed, t + 1)
                else:
                    pe.wait_ge(exp_sparse, t + 1)
                acquire(pe, "turn", t, n)
                for j in range(CC if n == 2 else CT):
                    src = p_comp[:, t % 3, j * P:(j + 1) * P] if n == 2 else \
                        p_sparse[:, t % 4, (n * CT + j) * P:(n * CT + j + 1) * P]
                    last = turned(bank("turn", t, n)[:, j * P:(j + 1) * P], src)
                last.then_inc(fill_sem("turn", t, n), 1)

            def attend(t):
                b = t // TB
                acquire(pe, "attend", t)
                for c in range(b * CB, (b + 1) * CB):
                    await_drain(pe, "vo", c)
                await_drain(pe, "vco", b)
                for n in (2, 0, 1):
                    await_drain(pe, "turn", t, n)
                    for j in range(CC if n == 2 else CT):
                        k = n * CT + j
                        v = vco[:, b * CC + j, :] if n == 2 else vo[:, b * TB + k, :]
                        last = mm(bank("attend", t)[:, 0:D], pT[:, t % 2, k * P:(k + 1) * P], v,
                                  start=(k == TB), stop=(k == TB - 1))
                last.then_inc(fill_sem("attend", t), 1)

            own = {"warm_up": warm_up, "xnT": xnT_, "Q": lambda c: project("Q", 0, c), "K": lambda c: project("K", 1, c),
                   "V": lambda c: project("V", 2, c), "moment": moment, "cq": cq, "muvar": muvar, "raw": raw, "vo": vo_,
                   "vco": vco_, "ffn_weights": ffn_weights, "gate": gate, "up": up, "down": down, "check": check,
                   "turn": turn, "attend": attend}
            for stage, *a in tensor_order:
                own[stage](*a)

        @block.scalar
        def _(act):
            a_ = nc.scalar.activation

            def xnT_(c):
                await_fill(act, "xnT", c)
                a_(xnT[:, c * CW:(c + 1) * CW], bank("xnT", c)[:, :], ACT.Copy).then_inc(drain_sem("xnT", c), 1)

            def K(c):
                await_fill(act, "K", c)
                act.wait_ge(w_loaded, 16 * 5)
                a_(kT[:, c * CW:(c + 1) * CW], bank("K", c)[:, :], ACT.Identity, bias=b_in[:, 1:2],
                   accum_out=ksum[:, c:c + 1]).then_inc(drain_sem("K", c), 1)

            def Q(c):
                await_fill(act, "Q", c)
                act.wait_ge(qbias_ready, 1)
                a_(qT[:, c * CW:(c + 1) * CW], bank("Q", c)[:, :], ACT.Identity, bias=q_bias[:, 0:1],
                   scale=SCALE).then_inc(drain_sem("Q", c), 1)

            def V(c):
                await_fill(act, "V", c)
                act.wait_ge(w_loaded, 16 * 5)
                a_(vT[:, c * CW:(c + 1) * CW], bank("V", c)[:, :], ACT.Identity,
                   bias=b_in[:, 2:3]).then_inc(drain_sem("V", c), 1)

            def vo_(c):
                await_fill(act, "vo", c)
                a_(vo[:, c * CT:(c + 1) * CT, :], bank("vo", c)[:, :].rearrange("p (j d) -> p j d", d=D), ACT.Copy,
                   scale=1.0 / 3.0).then_inc(drain_sem("vo", c), 1)

            def vco_(b):
                await_fill(act, "vco", b)
                a_(vco[:, b * CC:(b + 1) * CC, :], bank("vco", b)[:, 0:CC * D].rearrange("p (j d) -> p j d", d=D),
                   ACT.Copy, scale=1.0 / (3.0 * COMP)).then_inc(drain_sem("vco", b), 1)

            def count(r, t):
                if r == 0:
                    act.wait_ge(half_drained[0], t + 1)
                    act.wait_ge(half_drained[1], t + 1)
                    act.wait_ge(thr_ready[0], t // CT + 1)
                else:
                    act.wait_ge(thr_ready[r], t + 1)
                if r == 2 and t >= 4:
                    act.wait_ge(near_done, t - 3)
                dst = sg[:, t % 4, :] if r == 2 else sg_skip[:, r, :]
                if r < 2 and t:
                    act.wait_ge(counted[r], t)
                a_(dst, scores[:, t % XR, :], ACT.Sign, bias=nthr[:, r, row_tile(t):row_tile(t) + 1], scale=1.0,
                   accum_out=signs[:, r, row_tile(t):row_tile(t) + 1]).then_inc(counted[r], 1)

            def softmax(t, which):
                r = row_tile(t)
                w = causal_width(t)
                if which == 2:
                    act.wait_ge(sparse_ready, t + 1)
                    act.wait_ge(nmax_sparse, t + 1)
                    a_(p_sparse[:, t % 4, :], p_sparse[:, t % 4, :], ACT.Exp, bias=nmax[:, r, 2:3],
                       accum_out=zsum[:, r, 2:3]).then_inc(exp_sparse, 1)
                    return
                if which == 0:
                    if t >= 3:
                        act.wait_ge(mixed, t - 2)
                    act.wait_ge(nmax_causal, t + 1)
                    a_(p_causal[:, t % 3, 0:w], scores[:, t % XR, 0:w], ACT.Exp, bias=nmax[:, r, 0:1],
                       accum_out=zsum[:, r, 0:1]).then_inc(exp_causal, 1)
                else:
                    if t >= 3:
                        await_fill(act, "turn", t - 3, 2)
                    act.wait_ge(comp_drained, t + 1)
                    a_(p_comp[:, t % 3, :], comp[:, t % CR, :], ACT.Exp, bias=nmax[:, r, 1:2], scale=-1.0,
                       accum_out=zsum[:, r, 1:2]).then_inc(exp_comp, 1)

            def turned(t, n):
                if t >= 2:
                    await_fill(act, "attend", t - 2)
                await_fill(act, "turn", t, n)
                w = CC * P if n == 2 else CT * P
                a_(pT[:, t % 2, n * CT * P:n * CT * P + w], bank("turn", t, n)[:, 0:w],
                   ACT.Copy).then_inc(drain_sem("turn", t, n), 1)

            def ffn_weights(n):
                await_fill(act, "ffn_weights", n)
                dst = (wT_gate[:, :], wT_up[:, :], wT_down[:, :, :].rearrange("p h d -> p (h d)"))[n]
                a_(dst, bank("ffn_weights", n)[:, 0:H], ACT.Copy,
                   scale=0.5 if n == 2 else 1.0).then_inc(drain_sem("ffn_weights", n), 1)

            def up(c, h):
                n = CHUNKS.index(c) * NH + h
                await_fill(act, "up", c, h)
                if n >= 2:
                    act.wait_ge(hid_ready, n - 1)
                a_(up_sb[:, n % 2, :], bank("up", c, h)[:, :], ACT.Copy).then_inc(drain_sem("up", c, h), 1)

            def gate(c, h):
                n = CHUNKS.index(c) * NH + h
                await_fill(act, "gate", c, h)
                if n >= 2:
                    act.wait_ge(hid_ready, n - 1)
                a_(tanh_g[:, n % 2, :], bank("gate", c, h)[:, :], ACT.Tanh, scale=0.5).then_inc(tanh_ready, 1)

            own = {"xnT": xnT_, "Q": Q, "K": K, "V": V, "ffn_weights": ffn_weights, "up": up, "vo": vo_,
                   "vco": vco_, "count": count, "softmax": softmax,
                   "turned": turned, "gate": gate}
            for stage, *a in parse(SCALAR_ORDER)[0]:
                own[stage](*a)

        @block.vector
        def _(dve):
            v = nc.vector
            steps = [0]

            def mark(ins):
                steps[0] += 1
                ins.then_inc(vec_step, 1)
                return steps[0]

            def chain(ins):
                dve.wait_ge(vec_step, mark(ins))

            def consts():
                v.memset(half_pow[:, 0, :], -0.5)
                v.memset(half_pow[:, 1, :], 0.5)
                v.memset(maxes[:, :, :], 0.0)
                for j in range(9):
                    v.memset(ramp[:, :, :, j:j + 1], float(j))
                v.memset(ones16[:, :], 1.0)
                v.memset(m9[:, :, 1, 8:9], 0.0)
                v.memset(ones[:, :], 1.0).then_inc(const_ready, 1)
                dve.wait_ge(const_ready, 1)

            def ln_stats(c):
                dve.wait_ge(x_loaded[c], 16)
                for t in range(c * CT, (c + 1) * CT):
                    last = v.bn_stats(bn[:, t, :], x_in[:, t, :])
                chain(last)
                for t in range(c * CT, (c + 1) * CT):
                    last = v.bn_aggr(mv[:, t, :], bn[:, t, :])
                last.then_inc(stats_ready, 1)

            def ln_apply(c):
                dve.wait_ge(rstd_ready, c + 1)
                for t in range(c * CT, (c + 1) * CT):
                    v.tensor_scalar(xn[:, t, :], x_in[:, t, :], mv[:, t, 0:1], rstd[:, t:t + 1], ALU.subtract,
                                    ALU.mult).then_inc(xn_ready, 1)

            def kbar_(b):
                for c in range(b * CB, (b + 1) * CB):
                    await_drain(dve, "K", c)
                chain(v.tensor_reduce(kbar_sum[:, b:b + 1], ksum[:, b * CB:(b + 1) * CB], AX_X, ALU.add))
                v.tensor_scalar(kbar[:, b:b + 1], kbar_sum[:, b:b + 1], 1.0 / S, None, ALU.mult).then_inc(kbar_ready, 1)

            def moment(b, n):
                await_fill(dve, "moment", b, n)
                if n == 0 and b:
                    await_fill(dve, "cq", CHUNKS[b * CB - 1])
                v.tensor_scalar(mom[:, n % 2, :], bank("moment", b, n)[:, 0:D], 1.0 / S if n == 0 else 1.0, None,
                                ALU.mult).then_inc(drain_sem("moment", b, n), 1)

            def cq(c):
                await_fill(dve, "cq", c)
                if c:
                    await_fill(dve, "muvar", CHUNK_BEFORE[c])
                v.tensor_tensor(qcq[:, :], bank("cq", c)[:, :], qT[:, c * CW:(c + 1) * CW],
                                ALU.mult).then_inc(drain_sem("cq", c), 1)

            def muvar(c):
                await_fill(dve, "muvar", c)
                v.tensor_copy(mu_var[:, c * CT:(c + 1) * CT, :],
                              bank("muvar", c)[:, 0:2 * CT].rearrange("p (j s) -> p j s", s=2)
                              ).then_inc(drain_sem("muvar", c), 1)

            def evac(t):
                r = row_tile(t)
                if t >= XR:
                    dve.wait_ge(exp_causal, t - XR + 1)
                cut, done = r % TB * P, set()
                for n, (a, b) in enumerate(pieces(t)):
                    h = a // HALF
                    if h not in done:
                        done.add(h)
                        dve.wait_ge(half_filled[h], t + 1)
                    ins = v.tensor_scalar(scores[:, t % XR, a:b], score_bank[h][:, a - h * HALF:b - h * HALF], 0.0,
                                          None, ALU.add, ALU.max, accum_out=maxes[:, r, 1 + n:2 + n])
                    if b in (HALF, S):
                        ins.then_inc(half_drained[h], 1)
                if t >= CR:
                    dve.wait_ge(exp_comp, t - CR + 1)
                dve.wait_ge(comp_filled, t + 1)
                v.tensor_scalar(comp[:, t % CR, :], comp_bank[:, 0:SC], -1.0 / COMP, None, ALU.mult, ALU.min,
                                accum_out=nmax[:, r, 1:2]).then_inc(comp_drained, 1)

            def hidden(c, h):
                n = CHUNKS.index(c) * NH + h
                await_fill(dve, "gate", c, h)
                dve.wait_ge(tanh_ready, n + 1)
                v.scalar_tensor_tensor(out=tanh_g[:, n % 2, :], in0=tanh_g[:, n % 2, :], scalar=1.0,
                                       in1=bank("gate", c, h)[:, :], op0=ALU.add,
                                       op1=ALU.mult).then_inc(drain_sem("gate", c, h), 1)

            def down_add(c):
                ts = slice(c * CT, (c + 1) * CT)
                await_fill(dve, "down", c)
                dve.wait_ge(xb_ready, c + 1)
                v.tensor_tensor(base[:, ts, :], bank("down", c)[:, :].rearrange("p (j d) -> p j d", d=D),
                                base[:, ts, :], ALU.add).then_inc(drain_sem("down", c), 1)

            def near_(p):
                ts = slice(row_tile(2 * p), row_tile(2 * p) + 2)
                dve.wait_ge(counted[2], 2 * p + 2)
                dve.wait_ge(thr_ready[2], 2 * p + 2)
                v.tensor_scalar(d_off[:, ts], signs[:, 2, ts], 0.5, MID, ALU.mult, ALU.add)
                chain(v.tensor_scalar(side2[:, ts], signs[:, 2, ts], -2 * MID, 2.0, ALU.is_gt, ALU.mult))
                v.tensor_scalar(nside[:, ts], side2[:, ts], -TINY, TINY, ALU.mult, ALU.add)
                chain(v.tensor_scalar(side[:, ts], side2[:, ts], -1.0, None, ALU.add))
                flipped = [mark(v.tensor_scalar(sg[:, t % 4, :], sg[:, t % 4, :],
                                                side[:, row_tile(t):row_tile(t) + 1], None, ALU.mult))
                           for t in (2 * p, 2 * p + 1)]
                v.tensor_tensor(sel[:, ts, 1], d_off[:, ts], side[:, ts], ALU.mult)
                v.tensor_tensor(tied[:, ts], side[:, ts], signs[:, 2, ts], ALU.mult)
                small = mark(v.scalar_tensor_tensor(out=m9[:, ts, 0, 0], in0=nthr[:, 2, ts], scalar=-1.0,
                                                    in1=nside[:, ts], op0=ALU.mult, op1=ALU.mult))
                for t in (2 * p, 2 * p + 1):
                    dve.wait_ge(vec_step, flipped[t % 2])
                    v.scalar_tensor_tensor(out=near[:, t % 2, :], in0=scores[:, t % XR, :],
                                           scalar=nside[:, row_tile(t):row_tile(t) + 1], in1=sg[:, t % 4, :], op0=ALU.mult,
                                           op1=ALU.min, accum_out=far[:, row_tile(t):row_tile(t) + 1]).then_inc(near_done, 1)
                dve.wait_ge(vec_step, small)
                v.scalar_tensor_tensor(out=sel[:, ts, 0], in0=side2[:, ts], scalar=0.5, in1=sel[:, ts, 1],
                                       op0=ALU.mult, op1=ALU.add).then_inc(pick_ready, 1)

            def pick_(p):
                ts = slice(row_tile(2 * p), row_tile(2 * p) + 2)
                dve.wait_ge(near_done, 2 * p + 1)
                v.max(m9[:, row_tile(2 * p), 0, 1:9], near[:, 0, :])
                dve.wait_ge(near_done, 2 * p + 2)
                found = mark(v.max(m9[:, row_tile(2 * p + 1), 0, 1:9], near[:, 1, :]))
                dve.wait_ge(pick_ready, p + 1)
                v.tensor_tensor(hot[:, :, :, :], ramp[:, :, :, :],
                                sel[:, ts, :].unsqueeze(3).to_broadcast([P, 2, 2, 9]), ALU.is_equal)
                first = mark(v.scalar_tensor_tensor(out=tied2[:, ts], in0=far[:, ts], scalar=2.0, in1=tied[:, ts],
                                                    op0=ALU.mult, op1=ALU.subtract))
                dve.wait_ge(vec_step, found)
                gaps = mark(v.tensor_tensor(m9[:, ts, 1, 0:8], m9[:, ts, 0, 0:8], m9[:, ts, 0, 1:9], ALU.subtract))
                dve.wait_ge(vec_step, first)
                v.tensor_scalar(tied[:, ts], tied2[:, ts], -float(S), None, ALU.is_equal)
                dve.wait_ge(vec_step, gaps)
                chain(v.tensor_tensor(hot_m[:, :, :, :], hot[:, :, :, :], m9[:, ts, :, :], ALU.mult))
                chain(v.tensor_reduce(picked[:, ts, :], hot_m[:, :, :, :], AX_X, ALU.add))
                v.scalar_tensor_tensor(out=tau[:, ts], in0=side[:, ts], scalar=-1.0 / TINY, in1=picked[:, ts, 0],
                                       op0=ALU.mult, op1=ALU.mult)
                v.scalar_tensor_tensor(out=good[:, ts], in0=picked[:, ts, 1], scalar=0.0, in1=tied[:, ts],
                                       op0=ALU.is_gt, op1=ALU.mult).then_inc(good_ready, 1)

            def verdict(p):
                await_fill(dve, "check", p)
                v.tensor_copy(n_good_i[0:1, p:p + 1], bank("check", p)[0:1, 0:1]).then_inc(drain_sem("check", p), 1)

            def sparse(p):
                pair = (2 * p, 2 * p + 1)
                ts = slice(row_tile(2 * p), row_tile(2 * p) + 2)
                if p >= 2:
                    for t in pair:
                        await_fill(dve, "turn", t - 4, 0)
                        await_fill(dve, "turn", t - 4, 1)
                v.tensor_reduce(nmax[:, ts, 2], maxes[:, ts, 1:5], AX_X, ALU.max, negate=True).then_inc(nmax_sparse, 2)
                await_drain(dve, "check", p)
                sure = dve.value_load(n_good_i[0:1, p:p + 1])
                with dve.If(sure == 2 * P):
                    for t in pair:
                        row = scores[:, t % XR, :]
                        v.scalar_tensor_tensor(out=p_sparse[:, t % 4, :], in0=row, scalar=tau[:, row_tile(t):row_tile(t) + 1], in1=row,
                                               op0=ALU.is_ge, op1=ALU.mult).then_inc(sparse_ready, 1)
                with dve.Else():
                    for t in pair:
                        row, taken = scores[:, t % XR, :], p_sparse[:, t % 4, :]
                        dve.drain()
                        v.tensor_copy(taken, row)
                        for r in range(TOP_K // 8):
                            dve.drain()
                            v.max(m9[:, row_tile(t), 0, 0:8], taken)
                            dve.drain()
                            v.match_replace(taken, m9[:, row_tile(t), 0, 0:8], taken, LOWEST)
                        dve.drain()
                        v.tensor_tensor(taken, taken, row, ALU.not_equal)
                        dve.drain()
                        v.tensor_tensor(taken, taken, row, ALU.mult).then_inc(sparse_ready, 1)

            def mask(t):
                r = row_tile(t)
                n_causal = sum(b <= r % TB * P for a, b in pieces(t))
                w = causal_width(t)
                diag = scores[:, t % XR, w - P:w]
                dve.wait_ge(sparse_ready, t + 1)
                if t == 0:
                    dve.wait_ge(ident_ready, 2)
                chain(v.tensor_tensor_reduce(out=diag, in0=diag, in1=causal[:, :], scale=1.0, scalar=MASKED,
                                             op0=ALU.add, op1=ALU.max, accum_out=maxes[:, r, 0:1]))
                v.tensor_reduce(nmax[:, r, 0:1], maxes[:, r, 0:1 + n_causal], AX_X, ALU.max,
                                negate=True).then_inc(nmax_causal, 1)

            def sums(t):
                r = row_tile(t)
                dve.wait_ge(exp_sparse, t + 1)
                dve.wait_ge(exp_causal, t + 1)
                dve.wait_ge(exp_comp, t + 1)
                v.reciprocal(zinv[:, r, :], zsum[:, r, :]).then_inc(zinv_ready, 1)

            def finish(t):
                r = row_tile(t)
                await_fill(dve, "attend", t)
                dve.wait_ge(zinv_ready, t + 1)
                await_drain(dve, "down", r // CT)
                v.scalar_tensor_tensor(out=base[:, r, :], in0=bank("attend", t)[:, 0:D],
                                       scalar=zinv[:, r, 2:3], in1=base[:, r, :], op0=ALU.mult,
                                       op1=ALU.add).then_inc(drain_sem("attend", t), 1)

            own = {"consts": consts, "ln_stats": ln_stats, "ln_apply": ln_apply, "kbar": kbar_,
                   "moment": moment, "cq": cq, "muvar": muvar, "evac": evac,
                   "hidden": hidden, "down_add": down_add,
                   "near": near_, "pick": pick_, "verdict": verdict,
                   "sparse": sparse, "mask": mask, "sums": sums, "finish": finish}
            for stage, *a in parse(VECTOR_ORDER)[0]:
                own[stage](*a)


_INS = ["L0_attn_x", "L0_attn_Wq", "L0_attn_bq", "L0_attn_Wk", "L0_attn_bk", "L0_attn_Wv", "L0_attn_bv",
        "L0_attn_Wo", "L0_attn_bo", "L0_ffn_w_gate", "L0_ffn_w_up", "L0_ffn_w_down"]


def kernel(**inputs):
    import numpy as np
    import concourse.bacc as bacc
    from concourse.bass_utils import run_bass_kernel_spmd

    nc = bacc.Bacc("TRN2", target_bir_lowering=False, num_devices=1)
    arrays, args = {}, []
    for name in _INS:
        a = np.ascontiguousarray(inputs[name])
        arrays[f"{name}_dram"] = a
        args.append(nc.dram_tensor(f"{name}_dram", a.shape, mybir.dt.from_np(a.dtype), kind="ExternalInput").ap())
    shape = arrays["L0_attn_x_dram"].shape
    out = nc.dram_tensor("out_dram", shape, F32, kind="ExternalOutput").ap()
    attention_ffn_block(nc, *args, out)
    r = run_bass_kernel_spmd(nc, [arrays], core_ids=[0])
    return r.results[0]["out_dram"]
```
